# Optimizing a Trainium2 kernel written in Bass

```python
import numpy as np
import jax
import jax.numpy as jnp

def _softmax(x, axis=-1):
    return jax.nn.softmax(x, axis=axis)

def _gelu(x):
    return jax.nn.gelu(x, approximate=True)

def _silu(x):
    return jax.nn.silu(x)

def _sigmoid(x):
    return jax.nn.sigmoid(x)

def _layernorm(x, axis=-1, eps=1e-05):
    m = jnp.mean(x, axis=axis, keepdims=True)
    v = jnp.var(x, axis=axis, keepdims=True)
    return (x - m) / jnp.sqrt(v + eps)

def _scatter_add(tgt, idx, src, axis=0):
    return tgt.at[idx].add(src)

def _segment_sum(src, seg, n):
    return jax.ops.segment_sum(src, seg, n)
kernel_name = 'mk_seq_preln_d1_jaxref_r8_ea5418'

def setup_inputs(seed: int=0):
    np.random.seed(seed)
    _w = jnp.asarray

    def _L0_attn_setup():
        import jax, jax.numpy as jnp
        import numpy as np
        key = jax.random.key(seed)
        ks = jax.random.split(key, 5)
        B, S, D = (1, 512, 256)
        H, Dh = (16, 128)
        scale = 1.0 / np.sqrt(D).astype(np.float32)
        return {'x': jax.random.normal(ks[0], (B, S, D), dtype=jnp.float32), 'W_K': jax.random.normal(ks[1], (H, Dh, D), dtype=jnp.float32) * scale, 'W_Q': jax.random.normal(ks[2], (H, Dh, D), dtype=jnp.float32) * scale, 'W_V': jax.random.normal(ks[3], (H, Dh, D), dtype=jnp.float32) * scale, 'W_O': jax.random.normal(ks[4], (D, H * Dh), dtype=jnp.float32) * scale}
    _L0_attn_in = _L0_attn_setup()

    def _L0_ffn_setup():
        import jax, jax.numpy as jnp
        import numpy as np
        E = 32
        G = 8
        TOPK_GROUP = 4
        K = 8
        SCALE = 2.5
        H = 256
        I = 128
        SI = 256

        def _route(x, router_weight, bias):
            T = x.shape[0]
            logits = jnp.einsum('th,eh->te', x.astype(jnp.float32), router_weight.astype(jnp.float32))
            scores = jax.nn.sigmoid(logits)
            sc = scores + bias
            grp = sc.reshape(T, G, E // G)
            group_scores = jax.lax.top_k(grp, 2)[0].sum(-1)
            gidx = jax.lax.top_k(group_scores, TOPK_GROUP)[1]
            gmask = jnp.zeros((T, G), sc.dtype).at[jnp.arange(T)[:, None], gidx].set(1.0)
            smask = jnp.repeat(gmask, E // G, axis=1)
            sc_masked = jnp.where(smask > 0, sc, 0.0)
            topk_idx = jax.lax.top_k(sc_masked, K)[1]
            topk_w = jnp.take_along_axis(scores, topk_idx, axis=1)
            topk_w = topk_w / (topk_w.sum(-1, keepdims=True) + 1e-20)
            topk_w = topk_w * SCALE
            return (topk_idx, topk_w)
        key = jax.random.key(seed)
        ks = jax.random.split(key, 9)
        B, S = (2, 256)
        std = 0.02
        return {'hidden_states': jax.random.normal(ks[0], (B, S, H), jnp.float32), 'router_weight': jax.random.normal(ks[1], (E, H), jnp.float32) * std, 'e_score_correction_bias': jnp.zeros((E,), jnp.float32), 'gate_proj': jax.random.normal(ks[2], (E, I, H), jnp.float32) * std, 'up_proj': jax.random.normal(ks[3], (E, I, H), jnp.float32) * std, 'down_proj': jax.random.normal(ks[4], (E, H, I), jnp.float32) * std, 'shared_gate': jax.random.normal(ks[5], (SI, H), jnp.float32) * std, 'shared_up': jax.random.normal(ks[6], (SI, H), jnp.float32) * std, 'shared_down': jax.random.normal(ks[7], (H, SI), jnp.float32) * std}
    _L0_ffn_in = _L0_ffn_setup()
    _d = {'L0_attn_x': _L0_attn_in['x'], 'L0_attn_W_K': _L0_attn_in['W_K'], 'L0_attn_W_Q': _L0_attn_in['W_Q'], 'L0_attn_W_V': _L0_attn_in['W_V'], 'L0_attn_W_O': _L0_attn_in['W_O'], 'L0_ffn_router_weight': _L0_ffn_in['router_weight'], 'L0_ffn_e_score_correction_bias': _L0_ffn_in['e_score_correction_bias'], 'L0_ffn_gate_proj': _L0_ffn_in['gate_proj'], 'L0_ffn_up_proj': _L0_ffn_in['up_proj'], 'L0_ffn_down_proj': _L0_ffn_in['down_proj'], 'L0_ffn_shared_gate': _L0_ffn_in['shared_gate'], 'L0_ffn_shared_up': _L0_ffn_in['shared_up'], 'L0_ffn_shared_down': _L0_ffn_in['shared_down']}
    _x0 = _d['L0_attn_x']
    _d['L0_attn_x'] = jax.random.normal(jax.random.fold_in(jax.random.key(seed), 1), (2, 1024, 256), dtype=_x0.dtype)
    del _x0
    return _d

def reference(L0_attn_x, L0_attn_W_K, L0_attn_W_Q, L0_attn_W_V, L0_attn_W_O, L0_ffn_router_weight, L0_ffn_e_score_correction_bias, L0_ffn_gate_proj, L0_ffn_up_proj, L0_ffn_down_proj, L0_ffn_shared_gate, L0_ffn_shared_up, L0_ffn_shared_down):

    def _L0_attn_ref(x, W_K, W_Q, W_V, W_O):
        import jax, jax.numpy as jnp
        import numpy as np
        b, pos, d_model = x.shape
        d_head = W_K.shape[1]
        k = jnp.einsum('ihd,bpd->biph', W_K, x)
        q = jnp.einsum('ihd,bpd->biph', W_Q, x)
        v = jnp.einsum('ihd,bpd->biph', W_V, x)
        scores = jnp.einsum('biph,biqh->biqp', k, q)
        mask = jnp.tril(jnp.ones((pos, pos), dtype=x.dtype))
        masked = scores * mask - jnp.float32(10000000000.0) * (1.0 - mask)
        attn = jax.nn.softmax(masked / jnp.sqrt(jnp.float32(d_head)), axis=-1)
        z = jnp.einsum('biqp,biph->biqh', attn, v)
        z_flat = jnp.transpose(z, (0, 2, 1, 3)).reshape(b, pos, -1)
        out = jnp.einsum('df,bqf->bqd', W_O, z_flat)
        return out

    def _L0_ffn_ref(hidden_states, router_weight, e_score_correction_bias, gate_proj, up_proj, down_proj, shared_gate, shared_up, shared_down):
        import jax, jax.numpy as jnp
        import numpy as np
        E = 32
        G = 8
        TOPK_GROUP = 4
        K = 8
        SCALE = 2.5
        H = 256
        I = 128
        SI = 256

        def _route(x, router_weight, bias):
            T = x.shape[0]
            logits = jnp.einsum('th,eh->te', x.astype(jnp.float32), router_weight.astype(jnp.float32))
            scores = jax.nn.sigmoid(logits)
            sc = scores + bias
            grp = sc.reshape(T, G, E // G)
            group_scores = jax.lax.top_k(grp, 2)[0].sum(-1)
            gidx = jax.lax.top_k(group_scores, TOPK_GROUP)[1]
            gmask = jnp.zeros((T, G), sc.dtype).at[jnp.arange(T)[:, None], gidx].set(1.0)
            smask = jnp.repeat(gmask, E // G, axis=1)
            sc_masked = jnp.where(smask > 0, sc, 0.0)
            topk_idx = jax.lax.top_k(sc_masked, K)[1]
            topk_w = jnp.take_along_axis(scores, topk_idx, axis=1)
            topk_w = topk_w / (topk_w.sum(-1, keepdims=True) + 1e-20)
            topk_w = topk_w * SCALE
            return (topk_idx, topk_w)
        B, S, Hd = hidden_states.shape
        x = hidden_states.reshape(-1, Hd)
        T = x.shape[0]
        topk_idx, topk_w = _route(x, router_weight, e_score_correction_bias)
        topk_w = topk_w.astype(x.dtype)
        coeff = jnp.zeros((T, E), x.dtype).at[jnp.arange(T)[:, None], topk_idx].add(topk_w)

        def body(acc, ws):
            g, u, d, c = ws
            h = jax.nn.silu(x @ g.T) * (x @ u.T)
            return (acc + c[:, None] * (h @ d.T), None)
        out, _ = jax.lax.scan(body, jnp.zeros_like(x), (gate_proj, up_proj, down_proj, coeff.T))
        shared = jax.nn.silu(x @ shared_gate.T) * (x @ shared_up.T) @ shared_down.T
        return (out + shared).reshape(B, S, Hd)
    x = L0_attn_x
    x = x + _L0_attn_ref(_layernorm(x, axis=-1), L0_attn_W_K, L0_attn_W_Q, L0_attn_W_V, L0_attn_W_O)
    x = x + _L0_ffn_ref(_layernorm(x, axis=-1), L0_ffn_router_weight, L0_ffn_e_score_correction_bias, L0_ffn_gate_proj, L0_ffn_up_proj, L0_ffn_down_proj, L0_ffn_shared_gate, L0_ffn_shared_up, L0_ffn_shared_down)
    return x

_drawn_inputs = setup_inputs


def setup_inputs(seed=0):
    import zlib

    import numpy as np

    out = dict(_drawn_inputs(seed))
    spreads = {'L0_ffn_e_score_correction_bias': (0.0, 0.8)}
    factors = {'L0_ffn_router_weight': 8.0,
     'L0_ffn_gate_proj': 5.846,
     'L0_ffn_up_proj': 5.78,
     'L0_ffn_down_proj': 5.789,
     'L0_ffn_shared_gate': 3.684,
     'L0_ffn_shared_up': 3.647,
     'L0_ffn_shared_down': 3.64}
    for name, (base, spread) in spreads.items():
        noise = np.random.default_rng([zlib.crc32(name.encode()), seed]).standard_normal(out[name].shape)
        drawn = base * np.exp(spread * noise) if base else spread * noise
        out[name] = jnp.asarray(drawn.astype(out[name].dtype))
    for name, factor in factors.items():
        out[name] = (out[name] * factor).astype(out[name].dtype)
    return out
```

```python
import concourse.bass as bass
import numpy as np
from concourse import mybir
from contextlib import ExitStack

F32 = mybir.dt.float32
F32R = mybir.dt.float32r
BF16 = mybir.dt.bfloat16
ALU = mybir.AluOpType
ACT = mybir.ActivationFunctionType
AX = mybir.AxisListType

P = 128
B, S, D = 2, 1024, 256
H, DH = 16, 128
E, I, SI = 32, 128, 256
G, TOPG, TOPK = 8, 4, 8
SCALE = 2.5
EPS = 1e-5
MASKED = -1.0e30
NEVER = -3.0e38
ND = D // P
NT = S // P
NQ = 512
NC = S // NQ
BC = NQ // P
PAIRS = H // 2
NORM_OWN = 3 * NT + 5
EX = E + SI // I

ORDER = """
T0.0 T0.1 R0.0 X V0.0 V0.1 T0.2 T0.3 R0.1 X V0.2 V0.3 R0.2 R0.3 W0.0 W0.1
X T1.0 T1.1 R1.0 R1.1 X T1.2 V1.0 T1.3 V1.1 R1.2 V1.2 T1.4 T1.5 R1.3 V1.3
T1.6 V1.4 T1.7 X V1.5 T2.0 V1.6 T2.1 V1.7 X T2.2 R2.0 R2.1 W1.0 W1.1 V2.0
V2.1 T2.3 X V2.2 V2.3 R2.2 R2.3 W2.0 W2.1 X T3.0 T3.1 R3.0 X V3.0 V3.1
T3.2 T3.3 X T3.4 V3.2 T3.5 R3.1 V3.3 T3.6 V3.4 T3.7 R3.2 V3.5 V3.6 V3.7 X
R3.3 W3.0 W3.1 X
"""
ORDER = [(w[0], *(int(i) for i in w[1:].split("."))) if w != "X" else ("X", 0, 0)
         for w in ORDER.split()]
PROJ = [(1, "q", 0), (1, "k", 0), (1, "q", 1), (1, "k", 1),
        (0, "q", 0), (0, "k", 0), (0, "q", 1), (0, "k", 1)] + [(None, "v", n) for n in range(NT // 2)]
X_OWN = 4
ROWS = 2 * NT
TRS = 2 * (BC + NT)
BANKED = TRS + 2 * 2 * NC


def layer(nc, x, w_a, w_b, w_o, router, bias, experts, out):
    with ExitStack() as ctx:
        def dram(name, shape):
            return nc.dram_tensor(name, shape, F32, kind="Internal").ap()

        coeff_dram = [dram(f"coeff_{b}", [EX, S]) for b in range(B)]
        acc = ctx.enter_context(nc.sbuf_tensor("acc", [P, B * NT, D], F32))
        xT_hi = ctx.enter_context(nc.sbuf_tensor("xT_hi", [P, ND, B * S], F32R))
        xT_lo = ctx.enter_context(nc.sbuf_tensor("xT_lo", [P, ND, B * S], F32R))
        ident = ctx.enter_context(nc.sbuf_tensor("ident", [P, P], F32))
        with ExitStack() as part:
            attention(nc, part, x, w_a, w_b, w_o, acc, xT_hi, xT_lo, ident)
        with ExitStack() as part:
            mixture(nc, part, router, bias, experts, coeff_dram, acc, xT_hi, xT_lo, ident, out)


def flat(t):
    return t[:, :, :].rearrange("p a b -> p (a b)")


def norm_scratch(sb):
    return dict(stats=sb("stats", [P, NT, 6], F32), mv=sb("mv", [P, NT, 2], F32),
                std=sb("std", [P, NT], F32), inv=sb("inv", [P, NT], F32),
                tmp=sb("tmp", [P, NT], F32), var=sb("var", [P, NT], F32))


def norm_vector(dve, b, acc, xn, n, s_own, own, s_std_in, s_std_out, n_std):
    for t in range(NT):
        dve.bn_stats(n["stats"][:, t, :], acc[:, b * NT + t, :]).then_inc(s_own, 1)
    own += NT
    dve.wait_ge(s_own, own)
    for t in range(NT):
        dve.bn_aggr(n["mv"][:, t, :], n["stats"][:, t, :]).then_inc(s_own, 1)
    own += NT
    dve.wait_ge(s_own, own)
    dve.tensor_scalar(n["var"][:, :], n["mv"][:, :, 1], EPS, None, ALU.add).then_inc(s_std_in, 1)
    dve.wait_ge(s_std_out, n_std)
    dve.reciprocal(n["inv"][:, :], n["std"][:, :]).then_inc(s_own, 1)
    own += 1
    dve.wait_ge(s_own, own)
    dve.tensor_tensor(n["tmp"][:, :], n["inv"][:, :], n["inv"][:, :], ALU.mult).then_inc(s_own, 1)
    own += 1
    dve.wait_ge(s_own, own)
    dve.tensor_tensor(n["std"][:, :], n["tmp"][:, :], n["var"][:, :], ALU.mult).then_inc(s_own, 1)
    own += 1
    dve.wait_ge(s_own, own)
    dve.tensor_scalar(n["tmp"][:, :], n["std"][:, :], -0.5, 1.5, ALU.mult, ALU.add).then_inc(s_own, 1)
    own += 1
    dve.wait_ge(s_own, own)
    dve.tensor_tensor(n["var"][:, :], n["inv"][:, :], n["tmp"][:, :], ALU.mult).then_inc(s_own, 1)
    own += 1
    dve.wait_ge(s_own, own)
    for t in range(NT):
        last = dve.tensor_scalar(xn[:, t, :], acc[:, b * NT + t, :], n["mv"][:, t, 0:1],
                                 n["var"][:, t:t + 1], ALU.subtract, ALU.mult)
        last.then_inc(s_own, 1)
    own += NT
    return own


def attention(nc, ctx, x, w_a, w_b, w_o, acc, xT_hi, xT_lo, ident):
    def sb(name, shape, dt):
        return ctx.enter_context(nc.sbuf_tensor("at_" + name, shape, dt))

    def ps(name, shape):
        return ctx.enter_context(nc.psum_tensor("at_" + name, shape, F32))

    def sem(name):
        return ctx.enter_context(nc.semaphore("at_" + name))

    n_ = norm_scratch(sb)
    xn = sb("xn", [P, NT, D], F32)
    ident_bf = sb("ident_bf", [P, P], BF16)
    causal = sb("causal", [P, P], BF16)
    raw_a, a_hi, a_lo = sb("raw_a", [P, 1024], F32), sb("a_hi", [P, 1024], F32R), sb("a_lo", [P, 1024], F32R)
    raw_b, b_hi, b_lo = sb("raw_b", [P, 512], F32), sb("b_hi", [P, 512], F32R), sb("b_lo", [P, 512], F32R)
    raw_o = [sb(f"raw_o{a}", [P, D], F32) for a in range(2)]
    o_hi = [sb(f"o_hi{a}", [P, D], F32R) for a in range(2)]
    o_lo = [sb(f"o_lo{a}", [P, D], F32R) for a in range(2)]
    q_hi = [sb(f"q_hi{a}", [P, S], F32R) for a in range(2)]
    q_lo = [sb(f"q_lo{a}", [P, S], F32R) for a in range(2)]
    k_hi = [sb(f"k_hi{a}", [P, S], F32R) for a in range(2)]
    k_lo = [sb(f"k_lo{a}", [P, S], F32R) for a in range(2)]
    v_hi = [sb(f"v_hi{a}", [P, NT, DH], F32R) for a in range(2)]
    v_lo = [sb(f"v_lo{a}", [P, NT, DH], F32R) for a in range(2)]
    v_raw = sb("v_raw", [P, NT, DH], F32)
    prob = [sb(f"prob{c}", [P, BC, NQ * (c + 1)], F32) for c in range(NC)]
    pT_hi = [sb(f"pT_hi{n}", [P, NQ], F32R) for n in range(3)]
    pT_lo = [sb(f"pT_lo{n}", [P, NQ], F32R) for n in range(3)]
    pL_hi, pL_lo = sb("pL_hi", [P, 2 * P], F32R), sb("pL_lo", [P, 2 * P], F32R)
    z_hi, z_lo = sb("z_hi", [P, NQ], F32R), sb("z_lo", [P, NQ], F32R)
    zero = sb("zero", [P, 1], F32)
    neg_max = sb("neg_max", [P, NT], F32)
    row_sum = sb("row_sum", [P, NC, BC], F32)
    inv_sum = sb("inv_sum", [P, NC, BC], F32)

    ps_s = [ps(f"ps_s{n}", [P, S]) for n in range(2)]
    ps_t = [ps(f"ps_t{n}", [P, NQ]) for n in range(2)]
    ps_z = ps("ps_z", [P, NQ])
    ps_x = ps("ps_x", [P, NQ])

    s_load = [sem(f"load{b}") for b in range(B)]
    s_raw_a, s_raw_b = sem("raw_a"), sem("raw_b")
    s_raw_o = [sem(f"raw_o{a}") for a in range(2)]
    s_const = sem("const")
    s_own = sem("own")
    s_std_in, s_std_out = sem("std_in"), sem("std_out")
    s_xt, s_xt_hi, s_xt_lo = sem("xt"), sem("xt_hi"), sem("xt_lo")
    s_a, s_b, s_v1 = sem("split_a"), sem("split_b"), sem("split_v1")
    s_o = [sem(f"split_o{a}") for a in range(2)]
    s_pool = sem("pool_hi")
    s_scores, s_max, s_exp = sem("scores"), sem("max"), sem("exp")
    s_bank, s_hi, s_bank_free = sem("bank"), sem("pT_hi"), sem("bank_free")
    s_pv = sem("pv")
    s_x, s_x_hi, s_x_free = sem("x"), sem("x_hi"), sem("x_free")
    s_z_hi, s_z_lo = sem("z_hi"), sem("z_lo")
    s_inv = sem("inv_sum")
    EXP0, BANK0, PV0, X0 = 2, 2, 3, 1
    NX = len(PROJ)
    XT = 2 * B * NC

    block = ctx.enter_context(nc.Block())

    def walk():
        t = v = bank = n_x = 0
        for kind, k, n in ORDER:
            if kind in "TW":
                yield kind, k, n, bank
                bank += 1
            elif kind == "V":
                yield kind, k, n, v
                v += 1
            elif kind == "X":
                yield kind, k, n_x, n_x
                n_x += 1
            else:
                yield kind, k, n, None

    def t_count(k, n):
        return [0, BC, BC + NT, 2 * BC + NT][k] + n

    def bank_use(k, n):
        return next(m for kind, *at, m in walk() if kind == "T" and at == [k, n])

    def next_chunk(k):
        return ((k + 1) // 2) % 2, (k + 1) % 2, k == 3

    def width(r):
        return P * (r + 1)

    @block.sync
    def _(sp):
        def load(b):
            sp.dma_start(acc[:, b * NT:(b + 1) * NT, :],
                         x[b].rearrange("(t p) d -> p t d", p=P)).then_inc(s_load[b], 16)

        load(0)
        sp.dma_start(raw_a[:, :], w_a[0]).then_inc(s_raw_a, 16)
        sp.dma_start(raw_b[:, :], w_b[0]).then_inc(s_raw_b, 16)
        sp.dma_start(raw_o[0][:, :], w_o[0]).then_inc(s_raw_o[0], 16)
        load(1)

        def pair(p, now, then):
            sp.wait_ge(s_a, p + 1)
            if then is not None:
                sp.dma_start(raw_a[:, :], w_a[then]).then_inc(s_raw_a, 16)
            sp.wait_ge(s_o[1], p + 1)
            sp.dma_start(raw_o[1][:, :], w_o[now * 2 + 1]).then_inc(s_raw_o[1], 16)
            sp.wait_ge(s_b, p + 1)
            if then is not None:
                sp.dma_start(raw_b[:, :], w_b[then]).then_inc(s_raw_b, 16)
            sp.wait_ge(s_o[0], p + 1)
            if then is not None:
                sp.dma_start(raw_o[0][:, :], w_o[then * 2]).then_inc(s_raw_o[0], 16)

        for b in range(B):
            with sp.Fori(0, PAIRS - 1) as i:
                pair(b * PAIRS + i, i, i + 1)
            pair(b * PAIRS + PAIRS - 1, PAIRS - 1, 0 if b == 0 else None)

    @block.gpsimd
    def _(pool):
        pool.memset(ident[:, :], 0.0).then_inc(s_const, 1)
        pool.memset(ident_bf[:, :], 0.0).then_inc(s_const, 1)
        pool.memset(causal[:, :], 0.0).then_inc(s_const, 1)
        pool.memset(pL_hi[:, 0:P].bitcast(F32), 0.0).then_inc(s_const, 1)
        pool.memset(pL_lo[:, 0:P].bitcast(F32), 0.0).then_inc(s_const, 1)
        pool.memset(zero[:, :], 0.0).then_inc(s_const, 1)
        pool.wait_ge(s_const, 6)
        for m in (ident, ident_bf):
            pool.affine_select(out=m[:, :], in_=m[:, :], compare_op=ALU.not_equal, fill=1.0,
                               base=0, pattern=[[-1, P]], channel_multiplier=1).then_inc(s_const, 1)
        pool.affine_select(out=causal[:, :], in_=causal[:, :], compare_op=ALU.is_ge, fill=MASKED,
                           base=0, pattern=[[-1, P]], channel_multiplier=1).then_inc(s_const, 1)

        def split(hi, lo, raw, count, done):
            pool.tensor_tensor(hi, raw, zero[:, 0:1].to_broadcast([P, raw.shape[-1]]),
                               ALU.add).then_inc(s_pool, 1)
            pool.wait_ge(s_pool, count + 1)
            pool.tensor_tensor(lo, raw, hi.bitcast(F32), ALU.subtract).then_inc(done, 1)

        pool.sem_inc(s_o[1], 1)
        pool.wait_ge(s_raw_a, 16)
        split(a_hi[:, :], a_lo[:, :], raw_a[:, :], 0, s_a)
        pool.wait_ge(s_raw_b, 16)
        split(b_hi[:, :], b_lo[:, :], raw_b[:, :], 1, s_b)
        pool.wait_ge(s_raw_o[0], 16)
        split(o_hi[0][:, :], o_lo[0][:, :], raw_o[0][:, :], 2, s_o[0])

        def pair(p, then):
            n = 5 * p + 3
            if then:
                pool.wait_ge(s_raw_a, 16 * p + 32)
                pool.wait_ge(s_x, p * NX + NX - X_OWN)
                split(a_hi[:, :], a_lo[:, :], raw_a[:, :], n, s_a)
            pool.wait_ge(s_x_free, X0 + p * NX + NX - X_OWN)
            pool.wait_ge(s_pv, PV0 + p * TRS)
            split(flat(v_hi[1]), flat(v_lo[1]), flat(v_raw), n + 1 if then else n, s_v1)
            pool.wait_ge(s_raw_o[1], 16 * p + 16)
            pool.wait_ge(s_bank, p * BANKED + 1)
            split(o_hi[1][:, :], o_lo[1][:, :], raw_o[1][:, :], n + 2 if then else n + 1, s_o[1])
            if then:
                pool.wait_ge(s_raw_b, 16 * p + 32)
                pool.wait_ge(s_x, p * NX + NX)
                split(b_hi[:, :], b_lo[:, :], raw_b[:, :], n + 3, s_b)
                pool.wait_ge(s_raw_o[0], 16 * p + 32)
                pool.wait_ge(s_pv, PV0 + p * TRS + t_count(2, 0) + 1)
                split(o_hi[0][:, :], o_lo[0][:, :], raw_o[0][:, :], n + 4, s_o[0])

        for b in range(B):
            with pool.Fori(0, PAIRS - 1) as i:
                pair(b * PAIRS + i, True)
            pair(b * PAIRS + PAIRS - 1, b == 0)

    @block.tensor
    def _(pe):
        pe.sem_inc(s_pv, PV0)
        pe.wait_ge(s_const, 9)
        for b in range(B):
            for d in range(ND):
                for c in range(NC):
                    n = (b * ND + d) * NC + c
                    if n >= 2:
                        pe.wait_ge(s_xt_lo, n - 1)
                    pe.wait_ge(s_own, (b + 1) * NORM_OWN)
                    for t in range(BC):
                        last = pe.transpose(ps_t[n % 2][:, t * P:(t + 1) * P],
                                            xn[:, c * BC + t, d * P:(d + 1) * P], ident[:, :])
                    last.then_inc(s_xt, 1)
        pe.wait_ge(s_xt_lo, XT)

        def three(out, w_hi, w_lo, m_hi, m_lo, start, stop):
            pe.matmul(out, w_hi, m_hi, start=start, stop=False)
            pe.matmul(out, w_hi, m_lo, start=False, stop=False)
            return pe.matmul(out, w_lo, m_hi, start=False, stop=stop)

        def project(b, n, x_use, weights):
            a, what, part = PROJ[n]
            pe.wait_ge(s_x_free, X0 + x_use)
            if a == 1:
                pe.wait_ge(s_b, weights)
                w_hi, w_lo = b_hi, b_lo
            else:
                pe.wait_ge(s_a, weights)
                w_hi, w_lo = a_hi, a_lo
            if what == "v":
                for j in range(2):
                    t = b * S + (2 * part + j) * P
                    for d in range(ND):
                        m = slice(512 + d * 2 * DH, 512 + (d + 1) * 2 * DH)
                        last = three(ps_x[:, j * 2 * DH:(j + 1) * 2 * DH],
                                     xT_hi[:, d, t:t + P], xT_lo[:, d, t:t + P],
                                     w_hi[:, m], w_lo[:, m], d == 0, d == ND - 1)
            else:
                at = 0 if what == "q" else ND * DH
                t = b * S + part * NQ
                for d in range(ND):
                    w = slice(at + d * DH, at + (d + 1) * DH)
                    last = three(ps_x[:, :], w_hi[:, w], w_lo[:, w], xT_hi[:, d, t:t + NQ],
                                 xT_lo[:, d, t:t + NQ], d == 0, d == ND - 1)
            last.then_inc(s_x, 1)

        def scores(a, r, row, x_need):
            pe.wait_ge(s_exp, row + EXP0 - 1)
            pe.wait_ge(s_x_free, X0 + x_need)
            q = slice(r * P, (r + 1) * P)
            dst = ps_s[r % 2]
            for k0 in range(0, width(r), NQ):
                k1 = max(min(width(r), k0 + NQ), k0 + 2 * P)
                diagonal = r * P < k1 and r * P >= k0
                last = three(dst[:, k0:k1], q_hi[a][:, q], q_lo[a][:, q], k_hi[a][:, k0:k1],
                             k_lo[a][:, k0:k1], True, not diagonal)
                if diagonal:
                    last = pe.matmul(dst[:, r * P:(r + 1) * P], ident_bf[:, :], causal[:, :],
                                     start=False, stop=True)
            last.then_inc(s_scores, 1)

        def transpose(c, n, bank, use, rows):
            pe.wait_ge(s_bank_free, use + BANK0 - 1)
            pe.wait_ge(s_exp, rows + EXP0)
            for j in range(max(n - c * BC, 0), BC):
                last = pe.transpose(bank[:, j * P:(j + 1) * P],
                                    prob[c][:, j, n * P:(n + 1) * P], ident[:, :])
            last.then_inc(s_bank, 1)

        def times_v(a, c, n, t, t_use):
            pe.wait_ge(s_bank_free, t_use + BANK0 + 1)
            diag = max(n - c * BC, 0)
            if diag == BC - 1:
                m_hi, m_lo, q0 = pL_hi[:, :], pL_lo[:, :], (BC - 2) * P
            else:
                q0 = diag * P
                m_hi, m_lo = pT_hi[t % 3][:, q0:], pT_lo[t % 3][:, q0:]
            three(ps_z[:, q0:], v_hi[a][:, n, :], v_lo[a][:, n, :], m_hi, m_lo, n == 0,
                  n == (c + 1) * BC - 1).then_inc(s_pv, 1)

        def project_out(a, n, bank, use, chunk, weights):
            pe.wait_ge(s_bank_free, use + BANK0 - 1)
            pe.wait_ge(s_z_lo, chunk)
            pe.wait_ge(s_o[a], weights)
            for j in range(2):
                q = slice((2 * n + j) * P, (2 * n + j + 1) * P)
                last = three(bank[:, j * D:(j + 1) * D], z_hi[:, q], z_lo[:, q],
                             o_hi[a][:, :], o_lo[a][:, :], True, True)
            last.then_inc(s_bank, 1)

        def pair(b, p, then):
            for kind, k, n, m in walk():
                a, c = k // 2, k % 2
                na, nc_, is_next = next_chunk(k)
                if kind == "X":
                    own = n < X_OWN
                    if not own and then is None:
                        continue
                    project(b if own else then, n, NX - X_OWN + p * NX + n,
                            p + 1 if own else p + 2)
                elif kind == "R":
                    if is_next and then is None:
                        continue
                    r = nc_ * BC + n
                    need = NX - X_OWN + p * NX + [0, 2, X_OWN, X_OWN + 2][k]
                    scores(na, r, (p + 1) * ROWS + r if is_next else p * ROWS + na * NT + r, need)
                elif kind == "T":
                    transpose(c, n, ps_t[m % 2], p * BANKED + m, p * ROWS + a * NT + (c + 1) * BC)
                elif kind == "V":
                    if a == 1 and n == 0:
                        pe.wait_ge(s_v1, p + 1)
                    times_v(a, c, n, m, p * BANKED + bank_use(k, n))
                else:
                    project_out(a, n, ps_t[m % 2], p * BANKED + m, p * 4 + k + 1, p + 1 if a == 0 else p + 2)

        for n in range(X_OWN, NX):
            project(0, n, n - X_OWN, 1)
        for r in range(BC):
            scores(0, r, r, NX - X_OWN)
        for b in range(B):
            with pe.Fori(0, PAIRS - 1) as i:
                pair(b, b * PAIRS + i, b)
            pair(b, b * PAIRS + PAIRS - 1, 1 if b == 0 else None)

    @block.scalar
    def _(act):
        act.sem_inc(s_exp, EXP0)
        for b in range(B):
            act.wait_ge(s_std_in, b + 1)
            act.activation(n_["std"][:, :], n_["var"][:, :], ACT.Sqrt).then_inc(s_std_out, 1)
            for d in range(ND):
                for c in range(NC):
                    n = (b * ND + d) * NC + c
                    act.wait_ge(s_xt, n + 1)
                    act.activation(xT_hi[:, d, b * S + c * NQ:b * S + (c + 1) * NQ],
                                   ps_t[n % 2][:, :], ACT.Copy).then_inc(s_xt_hi, 1)

        def project(n, x_use):
            a, what, part = PROJ[n]
            act.wait_ge(s_x, x_use + 1)
            if what == "v":
                src = ps_x[:, :].rearrange("p (t a h) -> p a t h", t=2, a=2)
                t = slice(2 * part, 2 * part + 2)
                act.activation(v_raw[:, t, :], src[:, 1], ACT.Copy)
                act.activation(v_hi[0][:, t, :], src[:, 0], ACT.Copy).then_inc(s_x_hi, 1)
            elif what == "q":
                act.activation(q_hi[a][:, part * NQ:(part + 1) * NQ], ps_x[:, :], ACT.Copy,
                               scale=DH ** -0.5).then_inc(s_x_hi, 1)
            else:
                act.activation(k_hi[a][:, part * NQ:(part + 1) * NQ], ps_x[:, :],
                               ACT.Copy).then_inc(s_x_hi, 1)

        def exponentials(r, row):
            act.wait_ge(s_max, row + 1)
            c, j = r // BC, r % BC
            act.activation(prob[c][:, j, 0:width(r)], ps_s[r % 2][:, 0:width(r)], ACT.Exp,
                           bias=neg_max[:, r:r + 1],
                           accum_out=row_sum[:, c, j:j + 1]).then_inc(s_exp, 1)

        def pair(p, then):
            for kind, k, n, m in walk():
                a, c = k // 2, k % 2
                na, nc_, is_next = next_chunk(k)
                if kind == "X":
                    if n >= X_OWN and not then:
                        continue
                    project(n, NX - X_OWN + p * NX + n)
                elif kind == "R":
                    if is_next and not then:
                        continue
                    r = nc_ * BC + n
                    exponentials(r, (p + 1) * ROWS + r if is_next else p * ROWS + na * NT + r)
                elif kind == "T":
                    t = t_count(k, n)
                    act.wait_ge(s_bank, p * BANKED + m + 1)
                    act.wait_ge(s_pv, p * TRS + t + PV0 - 2)
                    j = max(n - c * BC, 0)
                    dst = pL_hi[:, P:] if j == BC - 1 else pT_hi[t % 3][:, j * P:]
                    act.activation(dst, ps_t[m % 2][:, j * P:], ACT.Copy).then_inc(s_hi, 1)
                elif kind == "V" and n == (c + 1) * BC - 1:
                    act.wait_ge(s_pv, p * TRS + m + PV0 + 1)
                    act.activation(z_hi[:, :], ps_z[:, :], ACT.Copy).then_inc(s_z_hi, 1)

        for n in range(X_OWN, NX):
            project(n, n - X_OWN)
        for r in range(BC):
            exponentials(r, r)
        for b in range(B):
            with act.Fori(0, PAIRS - 1) as i:
                pair(b * PAIRS + i, True)
            pair(b * PAIRS + PAIRS - 1, b == 0)

    @block.vector
    def _(dve):
        dve.sem_inc(s_bank_free, BANK0)
        dve.sem_inc(s_x_free, X0)
        own = 0
        for b in range(B):
            dve.wait_ge(s_load[b], 16)
            if b > 0:
                dve.wait_ge(s_xt, b * ND * NC)
            own = norm_vector(dve, b, acc, xn, n_, s_own, own, s_std_in, s_std_out, b + 1)
            for d in range(ND):
                for c in range(NC):
                    n = (b * ND + d) * NC + c
                    at = slice(b * S + c * NQ, b * S + (c + 1) * NQ)
                    dve.wait_ge(s_xt_hi, n + 1)
                    dve.tensor_tensor(xT_lo[:, d, at], ps_t[n % 2][:, :],
                                      xT_hi[:, d, at].bitcast(F32), ALU.subtract).then_inc(s_xt_lo, 1)

        def project(n, x_use):
            a, what, part = PROJ[n]
            dve.wait_ge(s_x_hi, x_use + 1)
            if what == "v":
                src = ps_x[:, :].rearrange("p (t a h) -> p a t h", t=2, a=2)
                t = slice(2 * part, 2 * part + 2)
                dve.tensor_tensor(v_lo[0][:, t, :], src[:, 0], v_hi[0][:, t, :].bitcast(F32),
                                  ALU.subtract).then_inc(s_x_free, 1)
            elif what == "q":
                at = slice(part * NQ, (part + 1) * NQ)
                dve.scalar_tensor_tensor(q_lo[a][:, at], ps_x[:, :], DH ** -0.5,
                                         q_hi[a][:, at].bitcast(F32), ALU.mult,
                                         ALU.subtract).then_inc(s_x_free, 1)
            else:
                at = slice(part * NQ, (part + 1) * NQ)
                dve.tensor_tensor(k_lo[a][:, at], ps_x[:, :], k_hi[a][:, at].bitcast(F32),
                                  ALU.subtract).then_inc(s_x_free, 1)

        def maximum(r, row):
            dve.wait_ge(s_scores, row + 1)
            dve.tensor_reduce(neg_max[:, r:r + 1], ps_s[r % 2][:, 0:width(r)], AX.X, ALU.max,
                              negate=True).then_inc(s_max, 1)

        def pair(b, p, then):
            for kind, k, n, m in walk():
                a, c = k // 2, k % 2
                na, nc_, is_next = next_chunk(k)
                if kind == "X":
                    if n >= X_OWN and not then:
                        continue
                    project(n, NX - X_OWN + p * NX + n)
                elif kind == "R":
                    if is_next and not then:
                        continue
                    r = nc_ * BC + n
                    maximum(r, (p + 1) * ROWS + r if is_next else p * ROWS + na * NT + r)
                elif kind == "T":
                    t = t_count(k, n)
                    j = max(n - c * BC, 0)
                    last_block = j == BC - 1
                    hi = pL_hi[:, P:] if last_block else pT_hi[t % 3][:, j * P:]
                    lo = pL_lo[:, P:] if last_block else pT_lo[t % 3][:, j * P:]
                    dve.wait_ge(s_hi, p * TRS + t + 1)
                    dve.tensor_tensor(lo, ps_t[m % 2][:, j * P:], hi.bitcast(F32),
                                      ALU.subtract).then_inc(s_bank_free, 1)
                    if n == 0:
                        dve.reciprocal(inv_sum[:, c, :], row_sum[:, c, :]).then_inc(s_inv, 1)
                elif kind == "V" and n == (c + 1) * BC - 1:
                    dve.wait_ge(s_z_hi, p * 4 + k + 1)
                    dve.tensor_tensor(z_lo[:, :], ps_z[:, :], z_hi[:, :].bitcast(F32),
                                      ALU.subtract).then_inc(s_z_lo, 1)
                elif kind == "W":
                    dve.wait_ge(s_bank, p * BANKED + m + 1)
                    dve.wait_ge(s_inv, p * 4 + k + 1)
                    for j in range(2):
                        q = 2 * n + j
                        to = acc[:, b * NT + c * BC + q, :]
                        last = dve.scalar_tensor_tensor(
                            to, ps_t[m % 2][:, j * D:(j + 1) * D], inv_sum[:, c, q:q + 1],
                            to, ALU.mult, ALU.add)
                    last.then_inc(s_bank_free, 1)

        for n in range(X_OWN, NX):
            project(n, n - X_OWN)
        for r in range(BC):
            maximum(r, r)
        for b in range(B):
            with dve.Fori(0, PAIRS - 1) as i:
                pair(b, b * PAIRS + i, True)
            pair(b, b * PAIRS + PAIRS - 1, b == 0)


def mixture(nc, ctx, router, bias, experts, coeff_dram, acc, xT_hi, xT_lo, ident, out):
    def sb(name, shape, dt=F32):
        return ctx.enter_context(nc.sbuf_tensor("mx_" + name, shape, dt))

    def sem(name):
        return ctx.enter_context(nc.semaphore("mx_" + name))

    n_ = norm_scratch(sb)
    xn = sb("xn", [P, NT, D])
    rw = sb("router", [P, ND, E])
    bias_bc = sb("bias", [P, E])
    earlier = sb("earlier", [P, G, G])
    score = sb("score", [P, NT, E])
    biased = sb("biased", [P, NT, E])
    pair_a, pair_b, group = sb("pair_a", [P, NT, G]), sb("pair_b", [P, NT, G]), sb("group", [P, NT, G])
    above, level = sb("above", [P, NT, G, G]), sb("level", [P, NT, G, G])
    rank, kept = sb("rank", [P, NT, G]), sb("kept", [P, NT, G])
    best = sb("best", [P, NT, 8])
    taken = sb("taken", [P, NT, E])
    total, inv_total = sb("total", [P, NT]), sb("inv_total", [P, NT])
    coeff = sb("coeff", [P, NT, E])
    coT = sb("coT", [P, 2, P])
    ones = sb("ones", [EX - E, S])
    EW = 2 * ND * I + D
    GU = 2 * ND * I
    raw = [sb(f"raw{n}", [P, EW]) for n in range(2)]
    gu_hi = [sb(f"gu_hi{n}", [P, GU], F32R) for n in range(2)]
    gu_lo = [sb(f"gu_lo{n}", [P, GU], F32R) for n in range(2)]
    dn_hi = [sb(f"dn_hi{n}", [P, D], F32R) for n in range(2)]
    dn_lo = [sb(f"dn_lo{n}", [P, D], F32R) for n in range(2)]
    co = [sb(f"co{n}", [P, S]) for n in range(2)]
    sg = [sb(f"silu{n}", [P, NQ]) for n in range(2)]
    gated = [sb(f"gated{n}", [P, NQ]) for n in range(2)]
    h = [sb(f"h{n}", [P, NQ]) for n in range(2)]
    HB = 4
    h_hi = [sb(f"h_hi{n}", [P, NQ], F32R) for n in range(HB)]
    h_lo = [sb(f"h_lo{n}", [P, NQ], F32R) for n in range(HB)]
    zero = sb("zero", [P, 1])
    zeros = sb("zeros", [P, P], F32R)
    oT = sb("oT", [P, ND, S])

    ps_gu = [[ctx.enter_context(nc.psum_tensor(f"mx_gu{n}{m}", [P, NQ], F32)) for m in range(2)]
             for n in range(2)]
    ps_o = [[ctx.enter_context(nc.psum_tensor(f"mx_o{c}{d}", [P, NQ], F32)) for d in range(ND)]
            for c in range(NC)]

    s_const, s_in, s_ones = sem("const"), sem("in"), sem("ones")
    s_raw = [sem(f"raw{n}") for n in range(2)]
    s_co_in = [sem(f"co_in{n}") for n in range(2)]
    s_own, s_route = sem("own"), sem("route")
    s_std_in, s_std_out = sem("std_in"), sem("std_out")
    s_xt, s_xt_hi, s_xt_lo = sem("xt"), sem("xt_hi"), sem("xt_lo")
    s_logit, s_score, s_coeff = sem("logit"), sem("score"), sem("coeff")
    s_coT, s_coT_sb, s_co_dram = sem("coT"), sem("coT_sb"), sem("co_dram")
    s_gu, s_silu, s_gu_free = sem("gu"), sem("silu"), sem("gu_free")
    s_gated, s_h, s_h_hi, s_h_lo, s_dn = sem("gated"), sem("h"), sem("h_hi"), sem("h_lo"), sem("dn")
    s_pool, s_gu_w, s_dn_w = sem("pool_hi"), sem("gu_w"), sem("dn_w")
    s_oT_act, s_oT_dve, s_oT_ps, s_final, s_out = sem("oT_act"), sem("oT_dve"), sem("oT_ps"), sem("final"), sem("out")
    GU0, DN0, GUF0 = 4, 4, 2
    UNITS = EX * NC
    BODIES = EX // 2
    BU = 2 * NC

    block = ctx.enter_context(nc.Block())

    @block.sync
    def _(sp):
        sp.dma_start(rw[:, :, :], router).then_inc(s_in, 16)
        sp.dma_start(bias_bc[:, :], bias.partition_broadcast(P)).then_inc(s_in, 16)
        sp.wait_ge(s_ones, 1)
        for b in range(B):
            sp.dma_start(coeff_dram[b][E:EX, :], ones[:, :]).then_inc(s_co_dram, 16)

        def load(b, e, e_all, n):
            sp.wait_ge(s_dn_w, e_all + 1)
            sp.dma_start(raw[n][:, :], experts[e]).then_inc(s_raw[n], 16)
            sp.wait_ge(s_h, e_all * NC + NC)
            sp.dma_start(co[n][:, :], coeff_dram[b][e].partition_broadcast(P)).then_inc(s_co_in[n], 16)

        for b in range(B):
            sp.wait_ge(s_co_dram, 16 * (2 + 4 * B))
            with sp.Fori(0, BODIES) as i:
                for n in range(2):
                    load(b, i * 2 + n, b * EX + i * 2 + n, n)

    @block.gpsimd
    def _(pool):
        pool.memset(ones[:, :], 1.0).then_inc(s_ones, 1)
        pool.memset(zeros[:, :].bitcast(F32), 0.0).then_inc(s_const, 1)
        pool.memset(earlier[:, :, :], 1.0).then_inc(s_const, 1)
        pool.memset(zero[:, :], 0.0).then_inc(s_const, 1)
        pool.wait_ge(s_const, 3)
        pool.affine_select(out=earlier[:, :, :], in_=earlier[:, :, :], compare_op=ALU.is_gt, fill=0.0,
                           base=0, pattern=[[1, G], [-1, G]], channel_multiplier=0).then_inc(s_const, 1)
        pool.sem_inc(s_gu_w, 2)
        pool.sem_inc(s_dn_w, 2)

        def split(hi, lo, src, count, done):
            pool.tensor_tensor(hi, src, zero[:, 0:1].to_broadcast([P, src.shape[-1]]),
                               ALU.add).then_inc(s_pool, 1)
            pool.wait_ge(s_pool, count + 1)
            pool.tensor_tensor(lo, src, hi.bitcast(F32), ALU.subtract).then_inc(done, 1)

        for b in range(B):
            with pool.Fori(0, BODIES) as i:
                for n in range(2):
                    e = b * EX + i * 2 + n
                    pool.wait_ge(s_raw[n], 16 * (b * BODIES + i) + 16)
                    pool.wait_ge(s_gu, e * NC + GU0 - 2)
                    split(gu_hi[n][:, :], gu_lo[n][:, :], raw[n][:, 0:GU], 2 * e, s_gu_w)
                    pool.wait_ge(s_dn, e * NC + DN0 - 2)
                    split(dn_hi[n][:, :], dn_lo[n][:, :], raw[n][:, GU:], 2 * e + 1, s_dn_w)

    @block.tensor
    def _(pe):
        pe.sem_inc(s_gu, GU0)
        pe.sem_inc(s_dn, DN0)
        pe.wait_ge(s_in, 32)
        pe.wait_ge(s_const, 4)
        for b in range(B):
            for d in range(ND):
                for c in range(NC):
                    n = (b * ND + d) * NC + c
                    if n >= 2:
                        pe.wait_ge(s_xt_lo, n - 1)
                    pe.wait_ge(s_own, (b + 1) * NORM_OWN)
                    for t in range(BC):
                        last = pe.transpose(ps_gu[n % 2][0][:, t * P:(t + 1) * P],
                                            xn[:, c * BC + t, d * P:(d + 1) * P], ident[:, :])
                    last.then_inc(s_xt, 1)
            pe.wait_ge(s_xt_lo, (b + 1) * ND * NC)
            for t in range(NT):
                at = slice(b * S + t * P, b * S + (t + 1) * P)
                for d in range(ND):
                    pe.matmul(ps_o[b][0][:, t * E:(t + 1) * E], xT_hi[:, d, at].bitcast(F32),
                              rw[:, d, :], start=d == 0, stop=False)
                    last = pe.matmul(ps_o[b][0][:, t * E:(t + 1) * E], xT_lo[:, d, at].bitcast(F32),
                                     rw[:, d, :], start=False, stop=d == ND - 1)
            last.then_inc(s_logit, 1)
            pe.wait_ge(s_coeff, b + 1)
            for j in range(2):
                last = pe.transpose(ps_o[b][1][:, j * P:(j + 1) * P],
                                    coeff[:, j * 4:(j + 1) * 4, :].rearrange("p t e -> p (t e)"),
                                    ident[:, :])
            last.then_inc(s_coT, 1)

        def three(out_, w_hi, w_lo, m_hi, m_lo, start, stop):
            pe.matmul(out_, w_hi, m_hi, start=start, stop=False)
            pe.matmul(out_, w_hi, m_lo, start=False, stop=False)
            return pe.matmul(out_, w_lo, m_hi, start=False, stop=stop)

        def gate_up(b, n, c, u, e):
            pe.wait_ge(s_gu_free, u + GUF0 - 1)
            pe.wait_ge(s_gu_w, e + 3)
            at = slice(b * S + c * NQ, b * S + (c + 1) * NQ)
            for m in range(2):
                for d in range(ND):
                    w = slice((m * ND + d) * I, (m * ND + d + 1) * I)
                    last = three(ps_gu[c][m][:, :], gu_hi[n][:, w], gu_lo[n][:, w],
                                 xT_hi[:, d, at], xT_lo[:, d, at], d == 0, d == ND - 1)
            last.then_inc(s_gu, 1)

        def down(n, c, u, e, stop):
            pe.wait_ge(s_h_lo, u + 1)
            pe.wait_ge(s_dn_w, e + 3)
            slot = (n * NC + c) % HB
            for d in range(ND):
                w = slice(d * P, (d + 1) * P)
                last = three(ps_o[c][d][:, :], dn_hi[n][:, w], dn_lo[n][:, w], h_hi[slot][:, :],
                             h_lo[slot][:, :], False, stop)
            last.then_inc(s_dn, 1)

        for c in range(NC):
            gate_up(0, 0, c, c, 0)
        for b in range(B):
            if b == 0:
                pe.wait_ge(s_coT_sb, B)
            else:
                pe.wait_ge(s_final, b * 2 * NC)
            for c in range(NC):
                for d in range(ND):
                    pe.matmul(ps_o[c][d][:, :], zeros[:, :], xT_hi[:, d, 0:NQ], start=True, stop=False)

            def body(i, last):
                for j in range(BU):
                    u = b * UNITS + i * BU + j
                    f = j + NC
                    if not last or f < BU:
                        gate_up(b, f // NC % 2, f % NC, u + NC, b * EX + i * 2 + f // NC)
                    elif b + 1 < B:
                        gate_up(b + 1, 0, f % NC, u + NC, (b + 1) * EX)
                    down(j // NC, j % NC, u, b * EX + i * 2 + j // NC, last and j >= NC)

            with pe.Fori(0, BODIES - 1) as i:
                body(i, False)
            body(BODIES - 1, True)
            for c in range(NC):
                pe.wait_ge(s_oT_act, b * NC + c + 1)
                pe.wait_ge(s_oT_dve, b * NC + c + 1)
                for half in range(2):
                    for t in range(2):
                        for d in range(ND):
                            q = c * NQ + (half * 2 + t) * P
                            last = pe.transpose(ps_o[c][half][:, t * D + d * P:t * D + (d + 1) * P],
                                                oT[:, d, q:q + P], ident[:, :])
                    last.then_inc(s_oT_ps, 1)

    @block.scalar
    def _(act):
        for b in range(B):
            act.wait_ge(s_std_in, b + 1)
            act.activation(n_["std"][:, :], n_["var"][:, :], ACT.Sqrt).then_inc(s_std_out, 1)
            for d in range(ND):
                for c in range(NC):
                    n = (b * ND + d) * NC + c
                    act.wait_ge(s_xt, n + 1)
                    act.activation(xT_hi[:, d, b * S + c * NQ:b * S + (c + 1) * NQ],
                                   ps_gu[n % 2][0][:, :], ACT.Copy).then_inc(s_xt_hi, 1)
            act.wait_ge(s_logit, b + 1)
            act.activation(score[:, :, :].rearrange("p t e -> p (t e)"), ps_o[b][0][:, 0:NT * E],
                           ACT.Sigmoid).then_inc(s_score, 1)
            act.wait_ge(s_coT, b + 1)
            act.activation(coT[:, :, :].rearrange("p j t -> p (j t)"), ps_o[b][1][:, 0:2 * P],
                           ACT.Copy).then_inc(s_coT_sb, 1)
            act.wait_ge(s_coT_sb, b + 1)
            for j in range(4):
                act.dma_start(coeff_dram[b][0:E, :].rearrange("e (h j t) -> e h j t", h=2, j=4)[:, :, j, :],
                              coT[j * E:(j + 1) * E, :, :]).then_inc(s_co_dram, 16)
            act.wait_ge(s_co_dram, 16 * (2 + 4 * (b + 1)))

        def high(c_slot, n, u):
            act.wait_ge(s_h, u + 1 + 2 * NC)
            act.wait_ge(s_dn, u + 1)
            act.activation(h_hi[c_slot][:, :], h[n][:, :], ACT.Copy).then_inc(s_h_hi, 1)

        def unit(slot, u, first=False):
            act.wait_ge(s_gu, u + 1 + GU0)
            act.activation(sg[slot % 2][:, :], ps_gu[slot % 2][0][:, :], ACT.Silu).then_inc(s_silu, 1)
            if not first:
                high((slot - 1) % HB, (slot - 1) % 2, u - 1)

        unit(0, 0, True)
        unit(1, 1)
        for b in range(B):
            with act.Fori(0, BODIES - 1) as i:
                for j in range(BU):
                    unit((j + NC) % HB, b * UNITS + i * BU + j + NC)
            for j in range(BU):
                u = b * UNITS + UNITS - BU + j + NC
                if j < BU - NC or b + 1 < B:
                    unit((j + NC) % HB, u)
                elif j == BU - NC:
                    high((j + NC - 1) % HB, (j + NC - 1) % 2, u - 1)
            act.wait_ge(s_dn, (b + 1) * UNITS + DN0)
            for c in range(NC):
                act.activation(oT[:, 0, c * NQ:(c + 1) * NQ], ps_o[c][0][:, :],
                               ACT.Copy).then_inc(s_oT_act, 1)
            act.wait_ge(s_final, (b + 1) * 2 * NC)
            act.dma_start(out[b].rearrange("(t p) d -> p t d", p=P),
                          acc[:, b * NT:(b + 1) * NT, :]).then_inc(s_out, 16)
        act.wait_ge(s_out, 16 * B)

    @block.vector
    def _(dve):
        dve.sem_inc(s_gu_free, GUF0)
        dve.sem_inc(s_h, 2 * NC)
        own = 0
        routed = 0

        def step(ins):
            nonlocal routed
            routed += 1
            ins.then_inc(s_route, 1)
            dve.wait_ge(s_route, routed)

        dve.wait_ge(s_in, 32)
        dve.wait_ge(s_const, 4)
        for b in range(B):
            if b > 0:
                dve.wait_ge(s_xt, b * ND * NC)
            own = norm_vector(dve, b, acc, xn, n_, s_own, own, s_std_in, s_std_out, b + 1)
            for d in range(ND):
                for c in range(NC):
                    n = (b * ND + d) * NC + c
                    at = slice(b * S + c * NQ, b * S + (c + 1) * NQ)
                    dve.wait_ge(s_xt_hi, n + 1)
                    dve.tensor_tensor(xT_lo[:, d, at], ps_gu[n % 2][0][:, :],
                                      xT_hi[:, d, at].bitcast(F32), ALU.subtract).then_inc(s_xt_lo, 1)
            dve.wait_ge(s_score, b + 1)
            step(dve.tensor_tensor(biased[:, :, :], score[:, :, :],
                                   bias_bc[:, :].unsqueeze(1).to_broadcast([P, NT, E]), ALU.add))
            m = biased[:, :, :].rearrange("p t (g k) -> p t g k", k=E // G)
            step(dve.tensor_tensor(pair_a[:, :, :], m[:, :, :, 0], m[:, :, :, 1], ALU.max))
            step(dve.tensor_tensor(pair_b[:, :, :], m[:, :, :, 2], m[:, :, :, 3], ALU.max))
            step(dve.tensor_tensor(group[:, :, :], pair_a[:, :, :], pair_b[:, :, :], ALU.add))
            step(dve.tensor_tensor(pair_a[:, :, :], m[:, :, :, 0], m[:, :, :, 1], ALU.add))
            step(dve.tensor_tensor(group[:, :, :], group[:, :, :], pair_a[:, :, :], ALU.max))
            step(dve.tensor_tensor(pair_b[:, :, :], m[:, :, :, 2], m[:, :, :, 3], ALU.add))
            step(dve.tensor_tensor(group[:, :, :], group[:, :, :], pair_b[:, :, :], ALU.max))
            other = group[:, :, :].unsqueeze(2).to_broadcast([P, NT, G, G])
            this = group[:, :, :].unsqueeze(3).to_broadcast([P, NT, G, G])
            step(dve.tensor_tensor(above[:, :, :, :], other, this, ALU.is_gt))
            step(dve.tensor_tensor(level[:, :, :, :], other, this, ALU.is_equal))
            step(dve.tensor_tensor(level[:, :, :, :], level[:, :, :, :],
                                   earlier[:, :, :].unsqueeze(1).to_broadcast([P, NT, G, G]), ALU.mult))
            step(dve.tensor_tensor(above[:, :, :, :], above[:, :, :, :], level[:, :, :, :], ALU.add))
            step(dve.reduce_sum(rank[:, :, :], above[:, :, :, :], AX.X))
            step(dve.tensor_scalar(kept[:, :, :], rank[:, :, :], TOPG - 0.5, None, ALU.is_lt))
            step(dve.tensor_tensor(m, m, kept[:, :, :].unsqueeze(3).to_broadcast([P, NT, G, E // G]),
                                   ALU.mult))
            step(dve.tensor_scalar(biased[:, :, :], biased[:, :, :], 0.0, None, ALU.add))
            for t in range(NT):
                last = dve.max(best[:, t, :], biased[:, t, :])
                if t < NT - 1:
                    last.then_inc(s_route, 1)
            routed += NT - 1
            step(last)
            for t in range(NT):
                last = dve.match_replace(taken[:, t, :], best[:, t, :], biased[:, t, :], NEVER)
                if t < NT - 1:
                    last.then_inc(s_route, 1)
            routed += NT - 1
            step(last)
            step(dve.tensor_scalar(taken[:, :, :], taken[:, :, :], NEVER, None, ALU.is_equal))
            step(dve.tensor_tensor(taken[:, :, :], taken[:, :, :], score[:, :, :], ALU.mult))
            step(dve.reduce_sum(total[:, :], taken[:, :, :], AX.X))
            step(dve.tensor_scalar(total[:, :], total[:, :], 1e-20, None, ALU.add))
            step(dve.reciprocal(inv_total[:, :], total[:, :]))
            step(dve.tensor_scalar(inv_total[:, :], inv_total[:, :], SCALE, None, ALU.mult))
            dve.tensor_tensor(coeff[:, :, :], taken[:, :, :],
                              inv_total[:, :].unsqueeze(2).to_broadcast([P, NT, E]),
                              ALU.mult).then_inc(s_coeff, 1)

        def low(slot, u):
            dve.wait_ge(s_h_hi, u + 1)
            dve.tensor_tensor(h_lo[slot][:, :], h[slot % 2][:, :], h_hi[slot][:, :].bitcast(F32),
                              ALU.subtract).then_inc(s_h_lo, 1)

        def unit(slot, u, e_of, first=False):
            k = slot % 2
            dve.wait_ge(s_silu, u + 1)
            dve.tensor_tensor(gated[k][:, :], sg[k][:, :], ps_gu[k][1][:, :],
                              ALU.mult).then_inc(s_gu_free, 1)
            if not first:
                low((slot - 1) % HB, u - 1)
            n = slot // NC
            dve.wait_ge(s_gu_free, u + GUF0 + 1)
            dve.wait_ge(s_co_in[n], 16 * e_of + 16)
            dve.tensor_tensor(h[k][:, :], gated[k][:, :], co[n][:, k * NQ:(k + 1) * NQ],
                              ALU.mult).then_inc(s_h, 1)

        unit(0, 0, 0, True)
        unit(1, 1, 0)
        for b in range(B):
            with dve.Fori(0, BODIES - 1) as i:
                for j in range(BU):
                    unit((j + NC) % HB, b * UNITS + i * BU + j + NC,
                         b * BODIES + i + (j + NC) // BU)
            for j in range(BU):
                u = b * UNITS + UNITS - BU + j + NC
                if j < BU - NC or b + 1 < B:
                    unit((j + NC) % HB, u, b * BODIES + BODIES - 1 + (j + NC) // BU)
                elif j == BU - NC:
                    low((j + NC - 1) % HB, u - 1)
            dve.wait_ge(s_dn, (b + 1) * UNITS + DN0)
            for c in range(NC):
                dve.tensor_copy(oT[:, 1, c * NQ:(c + 1) * NQ], ps_o[c][1][:, :]).then_inc(s_oT_dve, 1)
            for c in range(NC):
                for half in range(2):
                    t = b * NT + c * BC + half * 2
                    dve.wait_ge(s_oT_ps, b * 2 * NC + 2 * c + half + 1)
                    to = acc[:, t:t + 2, :].rearrange("p t d -> p (t d)")
                    dve.tensor_tensor(to, ps_o[c][half][:, :], to, ALU.add).then_inc(s_final, 1)


def kernel(**inputs):
    import concourse.bacc as bacc
    from concourse.bass_utils import run_bass_kernel_spmd

    def by_chunk(w):
        w = np.swapaxes(w, -1, -2)
        w = w.reshape(*w.shape[:-2], ND, P, w.shape[-1])
        return np.swapaxes(w, -3, -2)

    a = {k: np.asarray(v) for k, v in inputs.items()}
    wq, wk, wv = (by_chunk(a["L0_attn_W_" + n]) for n in "QKV")
    first = [w[0::2].reshape(PAIRS, P, ND * DH) for w in (wq, wk)]
    second = [w[1::2].reshape(PAIRS, P, ND * DH) for w in (wq, wk)]
    v2 = wv.reshape(PAIRS, 2, P, ND, DH).transpose(0, 2, 3, 1, 4).reshape(PAIRS, P, ND * 2 * DH)
    wo = a["L0_attn_W_O"].reshape(D, H, DH).transpose(1, 2, 0)

    def shared(w):
        return w.reshape(SI // I, I, D)

    gate = by_chunk(np.concatenate([a["L0_ffn_gate_proj"], shared(a["L0_ffn_shared_gate"])]))
    up = by_chunk(np.concatenate([a["L0_ffn_up_proj"], shared(a["L0_ffn_shared_up"])]))
    down = np.concatenate([a["L0_ffn_down_proj"].transpose(0, 2, 1),
                           shared(a["L0_ffn_shared_down"].T)])
    arrays = {
        "x": a["L0_attn_x"],
        "w_a": np.concatenate(first + [v2], axis=2),
        "w_b": np.concatenate(second, axis=2),
        "w_o": wo,
        "router": by_chunk(a["L0_ffn_router_weight"]),
        "bias": a["L0_ffn_e_score_correction_bias"],
        "experts": np.concatenate([gate.reshape(EX, P, ND * I), up.reshape(EX, P, ND * I), down],
                                  axis=2),
    }
    arrays = {f"{k}_dram": np.ascontiguousarray(v) for k, v in arrays.items()}
    nc = bacc.Bacc("TRN2", target_bir_lowering=False, num_devices=1)
    args = [nc.dram_tensor(k, v.shape, mybir.dt.from_np(v.dtype), kind="ExternalInput").ap()
            for k, v in arrays.items()]
    out = nc.dram_tensor("out_dram", (B, S, D), F32, kind="ExternalOutput").ap()
    layer(nc, *args, out)
    r = run_bass_kernel_spmd(nc, [arrays], core_ids=[0])
    return r.results[0]["out_dram"]
```

```python
import concourse.bass as bass
import numpy as np
from concourse import mybir
from contextlib import ExitStack

F32 = mybir.dt.float32
F32R = mybir.dt.float32r
BF16 = mybir.dt.bfloat16
ALU = mybir.AluOpType
ACT = mybir.ActivationFunctionType
AX = mybir.AxisListType

P = 128
B, S, D = 2, 1024, 256
H, DH = 16, 128
E, I, SI = 32, 128, 256
G, TOPG, TOPK = 8, 4, 8
SCALE = 2.5
EPS = 1e-5
MASKED = -1.0e30
NEVER = -3.0e38
ND = D // P
NT = S // P
NQ = 512
NC = S // NQ
BC = NQ // P
PAIRS = H // 2
EX = E + SI // I

PAIR = """
T0.0 T0.1 R0.0 X0 V0.0 V0.1 T0.2 T0.3 R0.1 X1 V0.2 V0.3 R0.2 R0.3 W0.0 W0.1
X2 T1.0 T1.1 R1.0 R1.1 X3 T1.2 V1.0 T1.3 V1.1 R1.2 V1.2 T1.4 T1.5 R1.3 V1.3
T1.6 V1.4 T1.7 X4 V1.5 T2.0 V1.6 T2.1 V1.7 X5 T2.2 R2.0 R2.1 W1.0 W1.1 V2.0
V2.1 T2.3 X6 V2.2 V2.3 R2.2 R2.3 W2.0 W2.1 X7 T3.0 T3.1 R3.0 X8 V3.0 V3.1
T3.2 T3.3 X9 T3.4 V3.2 T3.5 R3.1 V3.3 T3.6 V3.4 T3.7 R3.2 V3.5 V3.6 V3.7 X10
R3.3 W3.0 W3.1 X11
"""
START = """
N0.0 N0.1 N1.0 N1.1 N0.2 N0.3 Y0.0 Y0.1 N1.2 N1.3 X4 X5 X8 Y1.0 Y1.1 R3.0 R3.1 X9 R3.2 R3.3
X6 X7 X10 X11
"""
MIDDLE = """
T0.0 T0.1 N2.0 R0.0 X0 N2.1 V0.0 V0.1 T0.2 T0.3 R0.1 X1 N3.0 V0.2 V0.3 R0.2 N3.1 R0.3 W0.0 W0.1
N2.2 X2 N2.3 T1.0 T1.1 R1.0 R1.1 X3 N3.2 T1.2 Y2.0 V1.0 N3.3 T1.3 V1.1 R1.2 Y2.1 V1.2 T1.4 T1.5 R1.3 Y3.0 V1.3
T1.6 V1.4 T1.7 Y3.1 V1.5 X4 T2.0 V1.6 T2.1 V1.7 X5 T2.2 R2.0 R2.1 W1.0 W1.1 V2.0
V2.1 T2.3 X6 V2.2 V2.3 R2.2 R2.3 W2.0 W2.1 X7 T3.0 T3.1 R3.0 X8 V3.0 V3.1
T3.2 T3.3 X9 T3.4 V3.2 T3.5 R3.1 V3.3 T3.6 V3.4 T3.7 R3.2 V3.5 V3.6 V3.7 X10
R3.3 W3.0 W3.1 X11
"""
NEXT_TO_LAST = """
T0.0 R0.0 R0.1 N0.0 V0.0 N0.1 T0.1 X0 T0.2 R0.2 R0.3 V0.1 N0.2 T0.3 V0.2 X1 T1.0 V0.3 T1.1 N1.0
X2 W0.0 W0.1 N0.3 V1.0 X3 T1.2 T1.3 V1.1 Y0.0 T1.4 R1.0 R1.1 V1.2 N1.1 Y0.1 T1.5 V1.3 R1.2 N1.2
T1.6 V1.4 X4 T1.7 R1.3 R2.0 N1.3 X5 V1.5 T2.0 V1.6 V1.7 T2.1 Y1.0 R2.1 R2.2 W1.0 T2.2 X6 R2.3
W1.1 V2.0 T2.3 X7 V2.1 V2.2 V2.3 T3.0 Y1.1 R3.0 R3.1 W2.0 T3.1 L0 W2.1 T3.2 X8 V3.0 R3.2 G0.0
G0.1 T3.3 V3.1 T3.4 X9 V3.2 T3.5 G0.2 V3.3 T3.6 V3.4 T3.7 V3.5 V3.6 G0.3 V3.7 X10 R3.3 W3.0 W3.1
X11
"""
LAST_PAIR = """
T0.0 T0.1 R0.0 R0.1 G0.4 V0.0 T0.2 T0.3 X0 R0.2 R0.3 V0.1 G0.5 V0.2 X1 V0.3 T1.0 R1.0 R1.1 G0.6
W0.0 X2 R1.2 W0.1 T1.1 X3 T1.2 V1.0 T1.3 G0.7 V1.1 T1.4 V1.2 T1.5 R1.3 V1.3 G0.8 V1.4 T1.6 T1.7
R2.0 R2.1 G0.9 V1.5 G0.10 V1.6 T2.0 T2.1 V1.7 R2.2 R2.3 W1.0 W1.1 V2.0 V2.1 T2.2 T2.3 T3.0 V2.2
V2.3 T3.1 W2.0 W2.1 V3.0 T3.2 V3.1 N2.0 N2.1 T3.3 U0 T3.4 V3.2 N2.2 V3.3 T3.5 U1 V3.4 T3.6 V3.5
N2.3 T3.7 U2 V3.6 V3.7 Y2.0 U3 W3.0 W3.1 Y2.1 N3.0 N3.1 U4 Z0 N3.2 N3.3 D0 U5 Z1 D1 D2 Y3.0 D3
Y3.1 U6 L1 D4 D5 G1.0 G1.1 U7 U8 G1.2 U9 D6 G1.3 U10 G1.4 U11 G1.5 D7 D8 G1.6 G1.7 G1.8 U12 G1.9
D9 U13 D10 G1.10 D11
"""


def items(order):
    return [(w[0], *(int(i) for i in w[1:].split(".")), *([0] * ("." not in w))) for w in order.split()]


START, PAIR, MIDDLE = items(START), items(PAIR), items(MIDDLE)
NEXT_TO_LAST, LAST_PAIR = items(NEXT_TO_LAST), items(LAST_PAIR)
PROJ = [(1, "q", 0), (1, "k", 0), (1, "q", 1), (1, "k", 1),
        (0, "q", 0), (0, "k", 0), (0, "q", 1), (0, "k", 1)] + [(None, "v", n) for n in range(NT // 2)]
NX = len(PROJ)
X_OWN = 4
ROWS = 2 * NT
TRS = 2 * (BC + NT)
BANKED = TRS + 2 * 2 * NC
NP = B * PAIRS
STATS, APPLY = 2 * BC + 1, BC + 4
UNITS = EX * NC
BODIES = EX // 2
BU = 2 * NC
DONE_BODIES = 3


def flat(t):
    return t[:, :, :].rearrange("p a b -> p (a b)")


def walk(order):
    count = {"TW": 0, "V": 0, "XYL": 0}
    for kind, k, n in order:
        group = next((g for g in count if kind in g), None)
        yield kind, k, n, count.get(group)
        if group:
            count[group] += 1


def count_of(order, what):
    return next(m for *item, m in walk(order) if tuple(item) == what)


def t_count(k, n):
    return [0, BC, BC + NT, 2 * BC + NT][k] + n


def uses(order):
    return sum(kind in "XYL" for kind, _, _ in order)


def runs():
    result, x_before = [], uses(START)
    for first, end, order in [(0, PAIRS - 1, PAIR), (PAIRS - 1, PAIRS, MIDDLE), (PAIRS, NP - 2, PAIR),
                              (NP - 2, NP - 1, NEXT_TO_LAST), (NP - 1, NP, LAST_PAIR)]:
        result.append((first, end, order, x_before))
        x_before += (end - first) * uses(order)
    return result


RUNS = runs()


def each_pair(engine, pair):
    for first, end, order, x_before in RUNS:
        b = first // PAIRS
        if end - first == 1:
            pair(b, first, order, x_before)
        else:
            with engine.Fori(first, end) as p:
                pair(b, p, order, (p - first) * NX + x_before)


def norm_of(order, half):
    return half + B * NC if order in (NEXT_TO_LAST, LAST_PAIR) else half


def scored(k):
    return ((k + 1) // 2) % 2, (k + 1) % 2, k == 3


def width(r):
    return P * (r + 1)


def layer(nc, x, w_a, w_b, w_o, router, bias, experts, out):
    with ExitStack() as ctx:
        build(nc, ctx, x, w_a, w_b, w_o, router, bias, experts, out)


def build(nc, ctx, x, w_a, w_b, w_o, router, bias, experts, out):
    def sb(name, shape, dt=F32):
        return ctx.enter_context(nc.sbuf_tensor(name, shape, dt))

    def sem(name):
        return ctx.enter_context(nc.semaphore("s_" + name))

    coeff_dram = [nc.dram_tensor(f"coeff_{b}", [EX, S], F32, kind="Internal").ap() for b in range(B)]

    acc = sb("acc", [P, B * NT, D])
    xT_hi = sb("xT_hi", [P, ND, B * S], F32R)
    xT_lo = sb("xT_lo", [P, ND, B * S], F32R)
    ident, ident_bf = sb("ident", [P, P]), sb("ident_bf", [P, P], BF16)
    causal = sb("causal", [P, P], BF16)
    zero, neg_half = sb("zero", [P, 1]), sb("neg_half", [P, 1])
    xn = sb("xn", [P, NT, D])
    stats, mv = sb("stats", [P, 2, BC, 6]), sb("mv", [P, 2, BC, 2])
    var, inv = sb("var", [P, 2, BC]), sb("inv", [P, 2, BC])
    tmp, tmp2, scale = sb("tmp", [P, 2, BC]), sb("tmp2", [P, 2, BC]), sb("scale", [P, 2, BC])
    raw_a, a_hi, a_lo = sb("raw_a", [P, 1024]), sb("a_hi", [P, 1024], F32R), sb("a_lo", [P, 1024], F32R)
    raw_b, b_hi, b_lo = sb("raw_b", [P, 512]), sb("b_hi", [P, 512], F32R), sb("b_lo", [P, 512], F32R)
    raw_o = sb("raw_o", [P, 2, D])
    o_hi = [sb(f"o_hi{a}", [P, D], F32R) for a in range(2)]
    o_lo = [sb(f"o_lo{a}", [P, D], F32R) for a in range(2)]
    q_hi = [sb(f"q_hi{a}", [P, S], F32R) for a in range(2)]
    q_lo = [sb(f"q_lo{a}", [P, S], F32R) for a in range(2)]
    k_hi = [sb(f"k_hi{a}", [P, S], F32R) for a in range(2)]
    k_lo = [sb(f"k_lo{a}", [P, S], F32R) for a in range(2)]
    v_hi = [sb(f"v_hi{a}", [P, NT, DH], F32R) for a in range(2)]
    v_lo = [sb(f"v_lo{a}", [P, NT, DH], F32R) for a in range(2)]
    v_raw = sb("v_raw", [P, NT, DH])
    prob = [sb(f"prob{c}", [P, BC, NQ * (c + 1)]) for c in range(NC)]
    pT_hi = [sb(f"pT_hi{n}", [P, NQ], F32R) for n in range(3)]
    pT_lo = [sb(f"pT_lo{n}", [P, NQ], F32R) for n in range(3)]
    pL_hi, pL_lo = sb("pL_hi", [P, 2 * P], F32R), sb("pL_lo", [P, 2 * P], F32R)
    z_hi, z_lo = sb("z_hi", [P, NQ], F32R), sb("z_lo", [P, NQ], F32R)
    neg_max = sb("neg_max", [P, NT])
    row_sum, inv_sum = sb("row_sum", [P, NC, BC]), sb("inv_sum", [P, NC, BC])

    rw, bias_bc = sb("router_w", [P, ND, E]), sb("bias_bc", [P, E])
    earlier = sb("earlier", [P, G, G])
    score, biased = sb("score", [P, NT, E]), sb("biased", [P, NT, E])
    pair_a, pair_b, group = sb("pair_a", [P, NT, G]), sb("pair_b", [P, NT, G]), sb("group", [P, NT, G])
    rank, kept = sb("rank", [P, NT, G]), sb("kept", [P, NT, G])
    best, taken = sb("best", [P, NT, 8]), sb("taken", [P, NT, E])
    total, inv_total = sb("total", [P, NT]), sb("inv_total", [P, NT])
    coeff, coT = sb("coeff", [P, NT, E]), sb("coT", [P, NT, E])
    ones = sb("ones", [EX - E, NQ])
    GU = 2 * ND * I
    raw = [sb(f"raw{n}", [P, GU + D]) for n in range(2)]
    gu_hi = [sb(f"gu_hi{n}", [P, GU], F32R) for n in range(2)]
    gu_lo = [sb(f"gu_lo{n}", [P, GU], F32R) for n in range(2)]
    dn_hi = [sb(f"dn_hi{n}", [P, D], F32R) for n in range(2)]
    dn_lo = [sb(f"dn_lo{n}", [P, D], F32R) for n in range(2)]
    h = [sb(f"h{n}", [P, NQ]) for n in range(2)]
    rank_parts = [[t.rearrange("p (t g h) -> p t g h", g=G, h=G) for t in parts]
                  for parts in ([h[0][:, :], h[1][:, :]], [raw_b[:, :], flat(raw_o)])]
    co = [prob[0][:, 2 * n:2 * n + 2, :].rearrange("p a b -> p (a b)") for n in range(2)]
    oT = prob[1][:, 0:ND, :]
    sg = [raw_a[:, n * NQ:(n + 1) * NQ] for n in range(2)]
    gated = [flat(v_raw)[:, n * NQ:(n + 1) * NQ] for n in range(2)]
    HB = 4
    h_hi = [q_hi[n // 2][:, n % 2 * NQ:(n % 2 + 1) * NQ] for n in range(HB)]
    h_lo = [q_lo[n // 2][:, n % 2 * NQ:(n % 2 + 1) * NQ] for n in range(HB)]
    zeros = pL_hi[:, 0:P]

    ps_s = [ctx.enter_context(nc.psum_tensor(f"ps_s{n}", [P, S], F32)) for n in range(2)]
    ps_t = [ctx.enter_context(nc.psum_tensor(f"ps_t{n}", [P, NQ], F32)) for n in range(2)]
    ps_z = ctx.enter_context(nc.psum_tensor("ps_z", [P, NQ], F32))
    ps_x = ctx.enter_context(nc.psum_tensor("ps_x", [P, NQ], F32))
    ps_gu = [[ps_s[c][:, m * NQ:(m + 1) * NQ] for m in range(2)] for c in range(NC)]
    ps_o = [[ps_t[0][:, :], ps_t[1][:, :]], [ps_z[:, :], ps_x[:, :]]]

    def in_gu(order, kind, k):
        return order is LAST_PAIR and (kind, k) in (("Y", B * NC - 1), ("L", B - 1))

    def bank_of(order, kind, k, n):
        return ps_gu[NC - 1][n] if in_gu(order, kind, k) else ps_x[:, :]

    s_const, s_load = sem("const"), [sem(f"load{h}") for h in range(B * NC)]
    s_ones, s_in = sem("ones"), sem("in")
    s_raw_a, s_raw_b = sem("raw_a"), sem("raw_b")
    s_raw_o = [sem(f"raw_o{a}") for a in range(2)]
    s_stats, s_pow, s_apply = sem("stats"), sem("pow"), sem("apply")
    s_a, s_b, s_v1 = sem("split_a"), sem("split_b"), sem("split_v1")
    s_o = [sem(f"split_o{a}") for a in range(2)]
    s_pool = sem("pool_hi")
    s_scores, s_max, s_exp = sem("scores"), sem("max"), sem("exp")
    s_bank, s_hi, s_bank_free = sem("bank"), sem("pT_hi"), sem("bank_free")
    s_pv = sem("pv")
    s_x, s_x_hi, s_x_free = sem("x"), sem("x_hi"), sem("x_free")
    s_z_hi, s_z_lo = sem("z_hi"), sem("z_lo")
    s_inv = sem("inv_sum")
    s_route, s_coT, s_co_dram = sem("route"), sem("coT"), sem("co_dram")
    s_raw = [sem(f"raw{n}") for n in range(2)]
    s_co_in = [sem(f"co_in{n}") for n in range(2)]
    s_gu, s_silu, s_gu_free = sem("gu"), sem("silu"), sem("gu_free")
    s_h, s_h_hi, s_h_lo, s_dn = sem("h"), sem("h_hi"), sem("h_lo"), sem("dn")
    s_gu_w, s_dn_w = sem("gu_w"), sem("dn_w")
    s_oT_act, s_oT_dve, s_oT_ps = sem("oT_act"), sem("oT_dve"), sem("oT_ps")
    s_final, s_out = sem("final"), sem("out")
    EXP0, BANK0, PV0, X0, O0 = 2, 2, 3, 1, 1
    GU0, DN0, GUF0, W0, H0 = 4, 4, 2, 2, 2 * NC
    CONSTS = 12
    X_LOGITS = [X0 + RUNS[b - B][3] + count_of(RUNS[b - B][2], ("L", b, 0)) + 1 for b in range(B)]

    block = ctx.enter_context(nc.Block())

    @block.sync
    def _(sp):
        for half in range(B * NC):
            b, c = divmod(half, NC)
            at = b * NT + c * BC
            sp.dma_start(acc[:, at:at + BC, :],
                         x[b, c * NQ:(c + 1) * NQ, :].rearrange("(t p) d -> p t d", p=P))\
                .then_inc(s_load[half], 16)
        sp.dma_start(rw[:, :, :], router).then_inc(s_in, 16)
        sp.dma_start(bias_bc[:, :], bias.partition_broadcast(P)).then_inc(s_in, 16)
        sp.wait_ge(s_ones, 1)
        for b in range(B):
            for c in range(NC):
                sp.dma_start(coeff_dram[b][E:EX, c * NQ:(c + 1) * NQ], ones[:, 0:NQ])\
                    .then_inc(s_co_dram, 16)
        stored = 16 * B * NC

        def pair(p, now, then):
            sp.wait_ge(s_a, 2 * (p + 1))
            if then is not None:
                sp.dma_start(raw_a[:, :], w_a[then]).then_inc(s_raw_a, 16)
            sp.wait_ge(s_o[1], p + O0)
            sp.dma_start(raw_o[:, 1, :], w_o[now * 2 + 1]).then_inc(s_raw_o[1], 16)
            sp.wait_ge(s_b, p + 1)
            if then is not None:
                sp.dma_start(raw_b[:, :], w_b[then]).then_inc(s_raw_b, 16)
            sp.wait_ge(s_o[0], p + 1)
            if then is not None:
                sp.dma_start(raw_o[:, 0, :], w_o[then * 2]).then_inc(s_raw_o[0], 16)

        for b in range(B):
            with sp.Fori(0, PAIRS - 1) as i:
                pair(b * PAIRS + i, i, i + 1)
            pair(b * PAIRS + PAIRS - 1, PAIRS - 1, 0 if b == 0 else None)

        def store(b):
            nonlocal stored
            sp.wait_ge(s_coT, b + 1)
            to = coeff_dram[b][0:E, :].rearrange("e (t q r) -> q e t r", q=4, r=E)
            for q in range(4):
                sp.dma_start(to[q], coT[q * E:(q + 1) * E, :, :]).then_inc(s_co_dram, 16)
            stored += 16 * 4
            sp.wait_ge(s_co_dram, stored)

        def load_weights(b, i, n):
            sp.wait_ge(s_dn_w, b * EX + i * 2 + n - 1 + W0)
            sp.dma_start(raw[n][:, :], experts[i * 2 + n]).then_inc(s_raw[n], 16)

        def load_coefficients(b, i, n):
            sp.wait_ge(s_h, (b * EX + i * 2 + n - 1) * NC + H0)
            sp.dma_start(co[n], coeff_dram[b][i * 2 + n].partition_broadcast(P))\
                .then_inc(s_co_in[n], 16)

        def loads(b, i):
            for n in range(2):
                load_weights(b, i, n)
                load_coefficients(b, i, n)

        for i in range(2):
            for n in range(2):
                load_weights(0, i, n)
        store(0)
        sp.wait_ge(s_bank, (NP - 1) * BANKED + count_of(LAST_PAIR, ("T", 2, BC - 1)) + 1)
        for i in range(2):
            for n in range(2):
                load_coefficients(0, i, n)
        with sp.Fori(2, 6) as i:
            loads(0, i)
        store(1)
        with sp.Fori(6, BODIES) as i:
            loads(0, i)
        with sp.Fori(0, BODIES) as i:
            loads(1, i)

    @block.gpsimd
    def _(pool):
        pool.memset(ident[:, :], 0.0).then_inc(s_const, 1)
        pool.memset(neg_half[:, :], -0.5).then_inc(s_const, 1)
        pool.memset(zero[:, :], 0.0).then_inc(s_const, 1)
        pool.memset(ident_bf[:, :], 0.0).then_inc(s_const, 1)
        pool.memset(causal[:, :], 0.0).then_inc(s_const, 1)
        pool.wait_ge(s_const, 5)
        for m in (ident, ident_bf):
            pool.affine_select(out=m[:, :], in_=m[:, :], compare_op=ALU.not_equal, fill=1.0,
                               base=0, pattern=[[-1, P]], channel_multiplier=1).then_inc(s_const, 1)
        pool.affine_select(out=causal[:, :], in_=causal[:, :], compare_op=ALU.is_ge, fill=MASKED,
                           base=0, pattern=[[-1, P]], channel_multiplier=1).then_inc(s_const, 1)

        pool.sem_inc(s_o[1], O0)
        pool.sem_inc(s_gu_w, W0)
        pool.sem_inc(s_dn_w, W0)

        def split(hi, lo, src, count, done):
            pool.tensor_tensor(hi, src, zero[:, 0:1].to_broadcast([P, src.shape[-1]]),
                               ALU.add).then_inc(s_pool, 1)
            pool.wait_ge(s_pool, count + 1)
            pool.tensor_tensor(lo, src, hi.bitcast(F32), ALU.subtract).then_inc(done, 1)

        def power(q):
            pool.wait_ge(s_stats, (q + 1) * STATS)
            pool.tensor_tensor(inv[:, q % 2, :], var[:, q % 2, :],
                               neg_half[:, 0:1].to_broadcast([P, BC]), ALU.pow).then_inc(s_pow, 1)

        def split_a(count):
            for part in range(2):
                at = slice(part * 512, (part + 1) * 512)
                split(a_hi[:, at], a_lo[:, at], raw_a[:, at], count + part, s_a)

        power(0)
        pool.wait_ge(s_raw_a, 16)
        split_a(0)
        power(1)
        pool.wait_ge(s_raw_b, 16)
        split(b_hi[:, :], b_lo[:, :], raw_b[:, :], 2, s_b)
        pool.wait_ge(s_raw_o[0], 16)
        split(o_hi[0][:, :], o_lo[0][:, :], raw_o[:, 0, :], 3, s_o[0])
        pool.memset(pL_hi[:, 0:P].bitcast(F32), 0.0).then_inc(s_const, 1)
        pool.memset(pL_lo[:, 0:P].bitcast(F32), 0.0).then_inc(s_const, 1)
        pool.memset(ones[:, 0:NQ], 1.0).then_inc(s_ones, 1)
        pool.memset(earlier[:, :, :], 1.0).then_inc(s_const, 1)
        pool.wait_ge(s_const, 11)
        pool.affine_select(out=earlier[:, :, :], in_=earlier[:, :, :], compare_op=ALU.is_gt, fill=0.0,
                           base=0, pattern=[[1, G], [-1, G]], channel_multiplier=0).then_inc(s_const, 1)
        def split_v1(p, count, x_before):
            pool.wait_ge(s_x_free, x_before + X0)
            pool.wait_ge(s_pv, PV0 + p * TRS)
            split(flat(v_hi[1]), flat(v_lo[1]), flat(v_raw), count, s_v1)

        def split_o1(p, count):
            pool.wait_ge(s_raw_o[1], 16 * p + 16)
            pool.wait_ge(s_bank, p * BANKED + 1)
            split(o_hi[1][:, :], o_lo[1][:, :], raw_o[:, 1, :], count, s_o[1])

        def pair(_, p, order, x_before):
            n = 6 * p + 4
            if order is not LAST_PAIR:
                pool.wait_ge(s_raw_a, 16 * p + 32)
                pool.wait_ge(s_x, x_before)
                split_a(n)
                n += 2
                if order is MIDDLE:
                    power(2)
                    power(3)
                elif order is NEXT_TO_LAST:
                    power(4)
                    power(5)
            split_v1(p, n, x_before)
            split_o1(p, n + 1)
            if order is LAST_PAIR:
                return
            pool.wait_ge(s_raw_b, 16 * p + 32)
            pool.wait_ge(s_x, x_before + count_of(order, ("X", X_OWN - 1, 0)) + 1)
            split(b_hi[:, :], b_lo[:, :], raw_b[:, :], n + 2, s_b)
            pool.wait_ge(s_raw_o[0], 16 * p + 32)
            pool.wait_ge(s_pv, PV0 + p * TRS + t_count(2, 0) + 1)
            split(o_hi[0][:, :], o_lo[0][:, :], raw_o[:, 0, :], n + 3, s_o[0])

        each_pair(pool, pair)
        before = 6 * (NP - 1) + 6

        def gate_up(e, n, nth, count):
            pool.wait_ge(s_raw[n], 16 * nth + 16)
            pool.wait_ge(s_gu, (e - 1) * NC + GU0)
            split(gu_hi[n][:, :], gu_lo[n][:, :], raw[n][:, 0:GU], before + count, s_gu_w)

        def down(e, n, count):
            pool.wait_ge(s_dn, (e - 1) * NC + DN0)
            split(dn_hi[n][:, :], dn_lo[n][:, :], raw[n][:, GU:], before + count, s_dn_w)

        gate_up(0, 0, 0, 0)
        gate_up(1, 1, 0, 1)
        down(0, 0, 2)
        down(1, 1, 3)
        power(6)
        gate_up(2, 0, 1, 4)
        gate_up(3, 1, 1, 5)
        power(7)
        down(2, 0, 6)
        with pool.Fori(2, B * BODIES) as i:
            for n in range(2):
                e = i * 2 + n
                gate_up(e, n, i, 2 * e - 1)
                down(e - 1, 1 - n, 2 * e)
        down(B * EX - 1, 1, 2 * B * EX - 1)

    @block.tensor
    def _(pe):
        pe.sem_inc(s_pv, PV0)
        pe.sem_inc(s_gu, GU0)
        pe.sem_inc(s_dn, DN0)
        pe.wait_ge(s_const, 8)

        def three(to, w_hi, w_lo, m_hi, m_lo, start, stop):
            pe.matmul(to, w_hi, m_hi, start=start, stop=False)
            pe.matmul(to, w_hi, m_lo, start=False, stop=False)
            return pe.matmul(to, w_lo, m_hi, start=False, stop=stop)

        def transpose_xn(q, d, bank):
            for t in range(BC):
                pe.wait_ge(s_apply, (q + 1) * APPLY - BC + t + 1)
                last = pe.transpose(bank[:, t * P:(t + 1) * P],
                                    xn[:, q % NC * BC + t, d * P:(d + 1) * P], ident[:, :])
            last.then_inc(s_x, 1)

        def project(b, n, bank, weights):
            a, what, part = PROJ[n]
            if a == 1:
                pe.wait_ge(s_b, weights)
                w_hi, w_lo = b_hi, b_lo
            else:
                pe.wait_ge(s_a, weights)
                w_hi, w_lo = a_hi, a_lo
            if what == "v":
                for j in range(2):
                    t = b * S + (2 * part + j) * P
                    for d in range(ND):
                        m = slice(512 + d * 2 * DH, 512 + (d + 1) * 2 * DH)
                        last = three(bank[:, j * 2 * DH:(j + 1) * 2 * DH],
                                     xT_hi[:, d, t:t + P], xT_lo[:, d, t:t + P],
                                     w_hi[:, m], w_lo[:, m], d == 0, d == ND - 1)
            else:
                at = 0 if what == "q" else ND * DH
                t = b * S + part * NQ
                for d in range(ND):
                    w = slice(at + d * DH, at + (d + 1) * DH)
                    last = three(bank[:, :], w_hi[:, w], w_lo[:, w], xT_hi[:, d, t:t + NQ],
                                 xT_lo[:, d, t:t + NQ], d == 0, d == ND - 1)
            last.then_inc(s_x, 1)

        def scores(a, r, row, x_need):
            pe.wait_ge(s_exp, row + EXP0 - 1)
            pe.wait_ge(s_x_free, x_need + X0)
            q = slice(r * P, (r + 1) * P)
            to = ps_s[r % 2]
            for k0 in range(0, width(r), NQ):
                k1 = max(min(width(r), k0 + NQ), k0 + 2 * P)
                diagonal = k0 <= r * P < k1
                last = three(to[:, k0:k1], q_hi[a][:, q], q_lo[a][:, q], k_hi[a][:, k0:k1],
                             k_lo[a][:, k0:k1], True, not diagonal)
                if diagonal:
                    last = pe.matmul(to[:, r * P:(r + 1) * P], ident_bf[:, :], causal[:, :],
                                     start=False, stop=True)
            last.then_inc(s_scores, 1)

        def transpose(c, n, bank, use, rows):
            pe.wait_ge(s_bank_free, use + BANK0 - 1)
            pe.wait_ge(s_exp, rows + EXP0)
            for j in range(max(n - c * BC, 0), BC):
                last = pe.transpose(bank[:, j * P:(j + 1) * P], prob[c][:, j, n * P:(n + 1) * P],
                                    ident[:, :])
            last.then_inc(s_bank, 1)

        def times_v(a, c, n, t, t_use):
            pe.wait_ge(s_bank_free, t_use + BANK0 + 1)
            diag = max(n - c * BC, 0)
            if diag == BC - 1:
                m_hi, m_lo, q0 = pL_hi[:, :], pL_lo[:, :], (BC - 2) * P
            else:
                q0 = diag * P
                m_hi, m_lo = pT_hi[t % 3][:, q0:], pT_lo[t % 3][:, q0:]
            three(ps_z[:, q0:], v_hi[a][:, n, :], v_lo[a][:, n, :], m_hi, m_lo, n == 0,
                  n == (c + 1) * BC - 1).then_inc(s_pv, 1)

        def project_out(a, n, bank, use, chunk, weights):
            pe.wait_ge(s_bank_free, use + BANK0 - 1)
            pe.wait_ge(s_z_lo, chunk)
            pe.wait_ge(s_o[a], weights)
            for j in range(2):
                q = slice((2 * n + j) * P, (2 * n + j + 1) * P)
                last = three(bank[:, j * D:(j + 1) * D], z_hi[:, q], z_lo[:, q],
                             o_hi[a][:, :], o_lo[a][:, :], True, True)
            last.then_inc(s_bank, 1)

        def attend(kind, k, n, m, p, order, x_before):
            a, c = k // 2, k % 2
            if kind == "R":
                na, c_, is_next = scored(k)
                r = c_ * BC + n
                scores(na, r, (p + 1) * ROWS + r if is_next else p * ROWS + na * NT + r,
                       x_before - NT // 2 if k == 0 else
                       x_before + count_of(order, ("X", 2 * k - 1, 0)) + 1)
            elif kind == "T":
                transpose(c, n, ps_t[m % 2], p * BANKED + m, p * ROWS + a * NT + (c + 1) * BC)
            elif kind == "V":
                if a == 1 and n == 0:
                    pe.wait_ge(s_v1, p + 1)
                times_v(a, c, n, m, p * BANKED + count_of(order, ("T", k, n)))
            elif kind == "W":
                project_out(a, n, ps_t[m % 2], p * BANKED + m, p * 4 + k + 1,
                            p + 1 if a == 0 else p + 1 + O0)

        def logits(b, to):
            for t in range(NT):
                at = slice(b * S + t * P, b * S + (t + 1) * P)
                for d in range(ND):
                    pe.matmul(to[:, t * E:(t + 1) * E], xT_hi[:, d, at].bitcast(F32), rw[:, d, :],
                              start=d == 0, stop=False)
                    last = pe.matmul(to[:, t * E:(t + 1) * E], xT_lo[:, d, at].bitcast(F32),
                                     rw[:, d, :], start=False, stop=d == ND - 1)
            last.then_inc(s_x, 1)

        def gate_up(b, slot, u, e):
            n, c = slot // NC, slot % NC
            pe.wait_ge(s_gu_free, u + GUF0 - 1)
            pe.wait_ge(s_gu_w, e + 1 + W0)
            at = slice(b * S + c * NQ, b * S + (c + 1) * NQ)
            for m in range(2):
                for d in range(ND):
                    w = slice((m * ND + d) * I, (m * ND + d + 1) * I)
                    last = three(ps_gu[c][m], gu_hi[n][:, w], gu_lo[n][:, w],
                                 xT_hi[:, d, at], xT_lo[:, d, at], d == 0, d == ND - 1)
            last.then_inc(s_gu, 1)

        def down(slot, u, e, stop):
            n, c = slot // NC, slot % NC
            pe.wait_ge(s_h_lo, u + 1)
            pe.wait_ge(s_dn_w, e + 1 + W0)
            for d in range(ND):
                w = slice(d * P, (d + 1) * P)
                last = three(ps_o[c][d], dn_hi[n][:, w], dn_lo[n][:, w], h_hi[slot], h_lo[slot],
                             False, stop)
            last.then_inc(s_dn, 1)

        def clear(c):
            for d in range(ND):
                pe.matmul(ps_o[c][d], zeros, xT_hi[:, d, 0:NQ], start=True, stop=False)

        for kind, k, n, m in walk(START):
            bank = [ps_x, ps_z][(m or 0) % 2]
            if kind in "XY" and m >= 2:
                pe.wait_ge(s_x_free, X0 + m - 1)
            if kind == "Y":
                transpose_xn(k, n, bank)
            elif kind == "X":
                half = 1 if PROJ[k][1] != "v" and PROJ[k][2] == 1 or k >= X_OWN + 6 else 0
                pe.wait_ge(s_x_free, X0 + count_of(START, ("Y", half, ND - 1)) + 1)
                project(0, k, bank, 1 if k < X_OWN + 4 else 2)
            elif kind == "R":
                scores(0, n, n, count_of(START, ("X", X_OWN + 1, 0)) + 1)
        pe.wait_ge(s_x_free, X0 + uses(START))
        pe.wait_ge(s_const, CONSTS)
        pe.wait_ge(s_in, 32)

        def pair(b, p, order, x_before):
            then = 1 if order is MIDDLE else b
            ps_x_used = borrowed = units = 0
            for kind, k, n, m in walk(order):
                if kind in "XYL":
                    pe.wait_ge(s_x_free, x_before + m + X0)
                    if in_gu(order, kind, k):
                        pe.wait_ge(s_gu_free, GUF0 + units // NC * NC)
                        borrowed = m + 1
                    else:
                        ps_x_used = m + 1
                if kind == "X":
                    own = k < X_OWN
                    project(b if own else then, k, ps_x,
                            p + 1 if own else 2 * (p + 1) + (1 if k < X_OWN + 4 else 2))
                elif kind == "Y":
                    transpose_xn(norm_of(order, k), n, bank_of(order, kind, k, n))
                elif kind == "L":
                    logits(k, bank_of(order, kind, k, n))
                elif kind == "U":
                    if k < NC:
                        pe.wait_ge(s_exp, NP * ROWS + EXP0 - NC + 1 + k)
                    elif k % NC and borrowed:
                        pe.wait_ge(s_x_free, x_before + borrowed + X0)
                    gate_up(0, k % HB, k, k // NC)
                    units += 1
                elif kind == "Z":
                    if k == 0:
                        pe.wait_ge(s_bank_free, BANK0 + NP * BANKED)
                    else:
                        pe.wait_ge(s_x_free, x_before + ps_x_used + X0)
                    clear(k)
                elif kind == "D":
                    down(k % HB, k, k // NC, False)
                else:
                    attend(kind, k, n, m, p, order, x_before)

        each_pair(pe, pair)

        for b in range(B):
            if b > 0:
                pe.wait_ge(s_final, b * 2 * NC)
                for c in range(NC):
                    clear(c)

            def body(i, last):
                for j in range(BU):
                    u = b * UNITS + i * BU + j
                    f = j + NC
                    if not last or f < BU:
                        gate_up(b, f % HB, u + NC, b * EX + i * 2 + f // NC)
                    elif b + 1 < B:
                        gate_up(b + 1, f % HB, u + NC, (b + 1) * EX)
                    down(j, u, b * EX + i * 2 + j // NC, last and j >= NC)

            with pe.Fori(DONE_BODIES if b == 0 else 0, BODIES - 1) as i:
                body(i, False)
            body(BODIES - 1, True)
            for c in range(NC):
                pe.wait_ge(s_oT_act, b * NC + c + 1)
                pe.wait_ge(s_oT_dve, b * NC + c + 1)
                for half in range(2):
                    for t in range(2):
                        for d in range(ND):
                            q = c * NQ + (half * 2 + t) * P
                            last = pe.transpose(ps_o[c][half][:, t * D + d * P:t * D + (d + 1) * P],
                                                oT[:, d, q:q + P], ident[:, :])
                    last.then_inc(s_oT_ps, 1)

    @block.scalar
    def _(act):
        act.dma_start(raw_a[:, :], w_a[0]).then_inc(s_raw_a, 16)
        act.dma_start(raw_b[:, :], w_b[0]).then_inc(s_raw_b, 16)
        act.dma_start(raw_o[:, 0, :], w_o[0]).then_inc(s_raw_o[0], 16)
        act.sem_inc(s_exp, EXP0)

        def xn_high(half, d, bank, use):
            act.wait_ge(s_x, use + 1)
            act.activation(xT_hi[:, d, half * NQ:(half + 1) * NQ], bank[:, :],
                           ACT.Copy).then_inc(s_x_hi, 1)

        def project(n, bank, use):
            a, what, part = PROJ[n]
            act.wait_ge(s_x, use + 1)
            if what == "v":
                src = bank[:, :].rearrange("p (t a h) -> p a t h", t=2, a=2)
                t = slice(2 * part, 2 * part + 2)
                act.activation(v_raw[:, t, :], src[:, 1], ACT.Copy)
                act.activation(v_hi[0][:, t, :], src[:, 0], ACT.Copy).then_inc(s_x_hi, 1)
            elif what == "q":
                act.activation(q_hi[a][:, part * NQ:(part + 1) * NQ], bank[:, :], ACT.Copy,
                               scale=DH ** -0.5).then_inc(s_x_hi, 1)
            else:
                act.activation(k_hi[a][:, part * NQ:(part + 1) * NQ], bank[:, :],
                               ACT.Copy).then_inc(s_x_hi, 1)

        def exponentials(r, row):
            act.wait_ge(s_max, row + 1)
            c, j = r // BC, r % BC
            act.activation(prob[c][:, j, 0:width(r)], ps_s[r % 2][:, 0:width(r)], ACT.Exp,
                           bias=neg_max[:, r:r + 1],
                           accum_out=row_sum[:, c, j:j + 1]).then_inc(s_exp, 1)

        def attend(kind, k, n, m, p):
            c = k % 2
            if kind == "R":
                na, c_, is_next = scored(k)
                r = c_ * BC + n
                exponentials(r, (p + 1) * ROWS + r if is_next else p * ROWS + na * NT + r)
            elif kind == "T":
                t = t_count(k, n)
                act.wait_ge(s_bank, p * BANKED + m + 1)
                act.wait_ge(s_pv, p * TRS + t + PV0 - 2)
                j = max(n - c * BC, 0)
                to = pL_hi[:, P:] if j == BC - 1 else pT_hi[t % 3][:, j * P:]
                act.activation(to, ps_t[m % 2][:, j * P:], ACT.Copy).then_inc(s_hi, 1)
            elif kind == "V" and n == (c + 1) * BC - 1:
                act.wait_ge(s_pv, p * TRS + m + PV0 + 1)
                act.activation(z_hi[:, :], ps_z[:, :], ACT.Copy).then_inc(s_z_hi, 1)

        def high(slot, u):
            act.wait_ge(s_h, u + 1 + H0)
            act.wait_ge(s_dn, u + 1)
            act.activation(h_hi[slot], h[slot % 2][:, :], ACT.Copy).then_inc(s_h_hi, 1)

        def unit(slot, u, first=False):
            act.wait_ge(s_gu, u + 1 + GU0)
            act.activation(sg[slot % 2], ps_gu[slot % 2][0], ACT.Silu).then_inc(s_silu, 1)
            if not first:
                high((slot - 1) % HB, u - 1)

        for kind, k, n, m in walk(START):
            bank = [ps_x, ps_z][(m or 0) % 2]
            if kind == "Y":
                xn_high(k, n, bank, m)
            elif kind == "X":
                project(k, bank, m)
            elif kind == "R":
                exponentials(n, n)

        def pair(_, p, order, x_before):
            for kind, k, n, m in walk(order):
                if kind == "X":
                    project(k, ps_x, x_before + m)
                elif kind == "Y":
                    xn_high(k, n, bank_of(order, kind, k, n), x_before + m)
                elif kind == "L":
                    act.wait_ge(s_x, x_before + m + 1)
                    act.activation(flat(score), bank_of(order, kind, k, n)[:, 0:NT * E], ACT.Exp,
                                   scale=-1.0).then_inc(s_x_hi, 1)
                elif kind == "U":
                    unit(k % HB, k, k == 0)
                else:
                    attend(kind, k, n, m, p)

        each_pair(act, pair)

        for b in range(B):
            with act.Fori(DONE_BODIES if b == 0 else 0, BODIES - 1) as i:
                for j in range(BU):
                    unit((j + NC) % HB, b * UNITS + i * BU + j + NC)
            for j in range(BU):
                u = b * UNITS + UNITS - BU + j + NC
                if j < BU - NC or b + 1 < B:
                    unit((j + NC) % HB, u)
                elif j == BU - NC:
                    high((j + NC - 1) % HB, u - 1)
            act.wait_ge(s_dn, (b + 1) * UNITS + DN0)
            for c in range(NC):
                act.activation(oT[:, 0, c * NQ:(c + 1) * NQ], ps_o[c][0],
                               ACT.Copy).then_inc(s_oT_act, 1)
            act.wait_ge(s_final, (b + 1) * 2 * NC)
            act.dma_start(out[b].rearrange("(t p) d -> p t d", p=P),
                          acc[:, b * NT:(b + 1) * NT, :]).then_inc(s_out, 16)
        act.wait_ge(s_out, 16 * B)

    @block.vector
    def _(dve):
        dve.sem_inc(s_bank_free, BANK0)
        dve.sem_inc(s_x_free, X0)
        dve.sem_inc(s_gu_free, GUF0)
        dve.sem_inc(s_h, H0)

        def norm(q, stage):
            k, tile = q % 2, q % (B * NC) * BC
            if stage == 0 and q < B * NC:
                dve.wait_ge(s_load[q], 16)
            if stage < 2:
                own = q * STATS
                for t in range(2 * stage, 2 * stage + 2):
                    dve.bn_stats(stats[:, k, t, :], acc[:, tile + t, :]).then_inc(s_stats, 1)
                if stage == 1:
                    dve.wait_ge(s_stats, own + BC)
                    for t in range(BC):
                        dve.bn_aggr(mv[:, k, t, :], stats[:, k, t, :]).then_inc(s_stats, 1)
                    dve.wait_ge(s_stats, own + 2 * BC)
                    dve.tensor_scalar(var[:, k, :], mv[:, k, :, 1], EPS, None,
                                      ALU.add).then_inc(s_stats, 1)
                return
            if stage == 2:
                own = q * APPLY
                dve.wait_ge(s_pow, q + 1)
                dve.tensor_tensor(tmp[:, k, :], inv[:, k, :], inv[:, k, :],
                                  ALU.mult).then_inc(s_apply, 1)
                dve.wait_ge(s_apply, own + 1)
                dve.tensor_tensor(tmp2[:, k, :], tmp[:, k, :], var[:, k, :],
                                  ALU.mult).then_inc(s_apply, 1)
                dve.wait_ge(s_apply, own + 2)
                dve.tensor_scalar(tmp[:, k, :], tmp2[:, k, :], -0.5, 1.5, ALU.mult, ALU.add)\
                    .then_inc(s_apply, 1)
                dve.wait_ge(s_apply, own + 3)
                dve.tensor_tensor(scale[:, k, :], inv[:, k, :], tmp[:, k, :],
                                  ALU.mult).then_inc(s_apply, 1)
                dve.wait_ge(s_apply, own + 4)
            for t in range(2 * stage - 4, 2 * stage - 2):
                dve.tensor_scalar(xn[:, q % NC * BC + t, :], acc[:, tile + t, :], mv[:, k, t, 0:1],
                                  scale[:, k, t:t + 1], ALU.subtract, ALU.mult).then_inc(s_apply, 1)

        def xn_low(half, d, bank, use):
            at = slice(half * NQ, (half + 1) * NQ)
            dve.wait_ge(s_x_hi, use + 1)
            dve.tensor_tensor(xT_lo[:, d, at], bank[:, :], xT_hi[:, d, at].bitcast(F32),
                              ALU.subtract).then_inc(s_x_free, 1)

        def project(n, bank, use):
            a, what, part = PROJ[n]
            dve.wait_ge(s_x_hi, use + 1)
            if what == "v":
                src = bank[:, :].rearrange("p (t a h) -> p a t h", t=2, a=2)
                t = slice(2 * part, 2 * part + 2)
                dve.tensor_tensor(v_lo[0][:, t, :], src[:, 0], v_hi[0][:, t, :].bitcast(F32),
                                  ALU.subtract).then_inc(s_x_free, 1)
            elif what == "q":
                at = slice(part * NQ, (part + 1) * NQ)
                dve.scalar_tensor_tensor(q_lo[a][:, at], bank[:, :], DH ** -0.5,
                                         q_hi[a][:, at].bitcast(F32), ALU.mult,
                                         ALU.subtract).then_inc(s_x_free, 1)
            else:
                at = slice(part * NQ, (part + 1) * NQ)
                dve.tensor_tensor(k_lo[a][:, at], bank[:, :], k_hi[a][:, at].bitcast(F32),
                                  ALU.subtract).then_inc(s_x_free, 1)

        def maximum(r, row):
            dve.wait_ge(s_scores, row + 1)
            dve.tensor_reduce(neg_max[:, r:r + 1], ps_s[r % 2][:, 0:width(r)], AX.X, ALU.max,
                              negate=True).then_inc(s_max, 1)

        def attend(kind, k, n, m, b, p):
            a, c = k // 2, k % 2
            if kind == "R":
                na, c_, is_next = scored(k)
                r = c_ * BC + n
                maximum(r, (p + 1) * ROWS + r if is_next else p * ROWS + na * NT + r)
            elif kind == "T":
                t = t_count(k, n)
                j = max(n - c * BC, 0)
                hi = pL_hi[:, P:] if j == BC - 1 else pT_hi[t % 3][:, j * P:]
                lo = pL_lo[:, P:] if j == BC - 1 else pT_lo[t % 3][:, j * P:]
                dve.wait_ge(s_hi, p * TRS + t + 1)
                dve.tensor_tensor(lo, ps_t[m % 2][:, j * P:], hi.bitcast(F32),
                                  ALU.subtract).then_inc(s_bank_free, 1)
                if n == 0:
                    dve.reciprocal(inv_sum[:, c, :], row_sum[:, c, :]).then_inc(s_inv, 1)
            elif kind == "V" and n == (c + 1) * BC - 1:
                dve.wait_ge(s_z_hi, p * 4 + k + 1)
                dve.tensor_tensor(z_lo[:, :], ps_z[:, :], z_hi[:, :].bitcast(F32),
                                  ALU.subtract).then_inc(s_z_lo, 1)
            elif kind == "W":
                dve.wait_ge(s_bank, p * BANKED + m + 1)
                dve.wait_ge(s_inv, p * 4 + k + 1)
                for j in range(2):
                    q = 2 * n + j
                    to = acc[:, b * NT + c * BC + q, :]
                    last = dve.scalar_tensor_tensor(
                        to, ps_t[m % 2][:, j * D:(j + 1) * D], inv_sum[:, c, q:q + 1],
                        to, ALU.mult, ALU.add)
                last.then_inc(s_bank_free, 1)

        routed = 0

        def step(*instructions):
            nonlocal routed
            for instruction in instructions:
                instruction.then_inc(s_route, 1)
            routed += len(instructions)

        def ready():
            dve.wait_ge(s_route, routed)

        m4 = biased[:, :, :].rearrange("p t (g k) -> p t g k", k=E // G)

        def route(b, stage):
            if stage > 0:
                ready()
            if stage == 0:
                dve.wait_ge(s_x_free, X_LOGITS[b])
                step(dve.reciprocal(flat(score), flat(score)))
                ready()
                step(dve.tensor_tensor(biased[:, :, :], score[:, :, :],
                                       bias_bc[:, :].unsqueeze(1).to_broadcast([P, NT, E]), ALU.add))
            elif stage == 1:
                step(dve.tensor_tensor(pair_a[:, :, :], m4[:, :, :, 0], m4[:, :, :, 1], ALU.max),
                     dve.tensor_tensor(pair_b[:, :, :], m4[:, :, :, 2], m4[:, :, :, 3], ALU.max))
                ready()
                step(dve.tensor_tensor(group[:, :, :], pair_a[:, :, :], pair_b[:, :, :], ALU.add))
                ready()
                step(dve.tensor_tensor(pair_a[:, :, :], m4[:, :, :, 0], m4[:, :, :, 1], ALU.add),
                     dve.tensor_tensor(pair_b[:, :, :], m4[:, :, :, 2], m4[:, :, :, 3], ALU.add))
            elif stage == 2:
                step(dve.tensor_tensor(group[:, :, :], group[:, :, :], pair_a[:, :, :], ALU.max))
                ready()
                step(dve.tensor_tensor(group[:, :, :], group[:, :, :], pair_b[:, :, :], ALU.max))
            elif stage == 3:
                above, level = rank_parts[b]
                other = group[:, :, :].unsqueeze(2).to_broadcast([P, NT, G, G])
                this = group[:, :, :].unsqueeze(3).to_broadcast([P, NT, G, G])
                step(dve.tensor_tensor(above, other, this, ALU.is_gt),
                     dve.tensor_tensor(level, other, this, ALU.is_equal))
            elif stage == 4:
                above, level = rank_parts[b]
                step(dve.tensor_tensor(level, level,
                                       earlier[:, :, :].unsqueeze(1).to_broadcast([P, NT, G, G]),
                                       ALU.mult))
                ready()
                step(dve.tensor_tensor(above, above, level, ALU.add))
            elif stage == 5:
                step(dve.reduce_sum(rank[:, :, :], rank_parts[b][0], AX.X))
                ready()
                step(dve.tensor_scalar(kept[:, :, :], rank[:, :, :], TOPG - 0.5, None, ALU.is_lt))
                ready()
                step(dve.tensor_tensor(m4, m4, kept[:, :, :].unsqueeze(3)
                                       .to_broadcast([P, NT, G, E // G]), ALU.mult))
            elif stage == 6:
                step(dve.tensor_scalar(biased[:, :, :], biased[:, :, :], 0.0, None, ALU.add))
                ready()
                step(*[dve.max(best[:, t, :], biased[:, t, :]) for t in range(NT)])
            elif stage == 7:
                step(*[dve.match_replace(taken[:, t, :], best[:, t, :], biased[:, t, :], NEVER)
                       for t in range(NT)])
            elif stage == 8:
                step(dve.tensor_scalar(taken[:, :, :], taken[:, :, :], NEVER, None, ALU.is_equal))
                ready()
                step(dve.tensor_tensor(taken[:, :, :], taken[:, :, :], score[:, :, :], ALU.mult))
                ready()
                step(dve.reduce_sum(total[:, :], taken[:, :, :], AX.X))
            elif stage == 9:
                step(dve.tensor_scalar(total[:, :], total[:, :], 1e-20, None, ALU.add))
                ready()
                step(dve.reciprocal(inv_total[:, :], total[:, :]))
                ready()
                step(dve.tensor_scalar(inv_total[:, :], inv_total[:, :], SCALE, None, ALU.mult))
                ready()
                step(dve.tensor_tensor(coeff[:, :, :], taken[:, :, :],
                                       inv_total[:, :].unsqueeze(2).to_broadcast([P, NT, E]), ALU.mult))
            else:
                if b > 0:
                    dve.wait_ge(s_co_dram, 16 * (B * NC + 4 * b))
                dve.transpose(flat(coT), flat(coeff)).then_inc(s_coT, 1)

        def low(slot, u):
            dve.wait_ge(s_h_hi, u + 1)
            dve.tensor_tensor(h_lo[slot], h[slot % 2][:, :], h_hi[slot].bitcast(F32),
                              ALU.subtract).then_inc(s_h_lo, 1)

        def unit(slot, u, pairs, first=False):
            c = slot % NC
            dve.wait_ge(s_silu, u + 1)
            dve.tensor_tensor(gated[c], sg[c], ps_gu[c][1], ALU.mult).then_inc(s_gu_free, 1)
            if not first:
                low((slot - 1) % HB, u - 1)
            dve.wait_ge(s_gu_free, u + GUF0 + 1)
            dve.wait_ge(s_co_in[slot // NC], 16 * pairs + 16)
            dve.tensor_tensor(h[c][:, :], gated[c], co[slot // NC][:, c * NQ:(c + 1) * NQ],
                              ALU.mult).then_inc(s_h, 1)

        for kind, k, n, m in walk(START):
            bank = [ps_x, ps_z][(m or 0) % 2]
            if kind == "N":
                norm(k, n)
            elif kind == "Y":
                xn_low(k, n, bank, m)
            elif kind == "X":
                project(k, bank, m)
            elif kind == "R":
                maximum(n, n)
        dve.wait_ge(s_in, 32)
        dve.wait_ge(s_const, CONSTS)

        def pair(b, p, order, x_before):
            for kind, k, n, m in walk(order):
                if kind == "N":
                    if n == 0 and order is LAST_PAIR and k >= NC:
                        use = count_of(order, ("W", k, 1)) + 1
                        dve.wait_ge(s_bank_free, BANK0 + p * BANKED + use)
                    norm(norm_of(order, k), n)
                elif kind == "X":
                    project(k, ps_x, x_before + m)
                elif kind == "Y":
                    xn_low(k, n, bank_of(order, kind, k, n), x_before + m)
                elif kind == "L":
                    dve.wait_ge(s_x_hi, x_before + m + 1)
                    dve.tensor_scalar(flat(score), flat(score), 1.0, None,
                                      ALU.add).then_inc(s_x_free, 1)
                elif kind == "G":
                    route(k, n)
                elif kind == "U":
                    unit(k % HB, k, k // BU, k == 0)
                else:
                    attend(kind, k, n, m, b, p)

        each_pair(dve, pair)

        for b in range(B):
            with dve.Fori(DONE_BODIES if b == 0 else 0, BODIES - 1) as i:
                for j in range(BU):
                    unit((j + NC) % HB, b * UNITS + i * BU + j + NC,
                         b * BODIES + i + (j + NC) // BU)
            for j in range(BU):
                u = b * UNITS + UNITS - BU + j + NC
                if j < BU - NC or b + 1 < B:
                    unit((j + NC) % HB, u, b * BODIES + BODIES - 1 + (j + NC) // BU)
                elif j == BU - NC:
                    low((j + NC - 1) % HB, u - 1)
            dve.wait_ge(s_dn, (b + 1) * UNITS + DN0)
            for c in range(NC):
                dve.tensor_copy(oT[:, 1, c * NQ:(c + 1) * NQ], ps_o[c][1]).then_inc(s_oT_dve, 1)
            for c in range(NC):
                for half in range(2):
                    t = b * NT + c * BC + half * 2
                    dve.wait_ge(s_oT_ps, b * 2 * NC + 2 * c + half + 1)
                    to = acc[:, t:t + 2, :].rearrange("p t d -> p (t d)")
                    dve.tensor_tensor(to, ps_o[c][half], to, ALU.add).then_inc(s_final, 1)


def kernel(**inputs):
    import concourse.bacc as bacc
    from concourse.bass_utils import run_bass_kernel_spmd

    def by_chunk(w):
        w = np.swapaxes(w, -1, -2)
        w = w.reshape(*w.shape[:-2], ND, P, w.shape[-1])
        return np.swapaxes(w, -3, -2)

    a = {k: np.asarray(v) for k, v in inputs.items()}
    wq, wk, wv = (by_chunk(a["L0_attn_W_" + n]) for n in "QKV")
    first = [w[0::2].reshape(PAIRS, P, ND * DH) for w in (wq, wk)]
    second = [w[1::2].reshape(PAIRS, P, ND * DH) for w in (wq, wk)]
    v2 = wv.reshape(PAIRS, 2, P, ND, DH).transpose(0, 2, 3, 1, 4).reshape(PAIRS, P, ND * 2 * DH)
    wo = a["L0_attn_W_O"].reshape(D, H, DH).transpose(1, 2, 0)

    def shared(w):
        return w.reshape(SI // I, I, D)

    gate = by_chunk(np.concatenate([a["L0_ffn_gate_proj"], shared(a["L0_ffn_shared_gate"])]))
    up = by_chunk(np.concatenate([a["L0_ffn_up_proj"], shared(a["L0_ffn_shared_up"])]))
    down = np.concatenate([a["L0_ffn_down_proj"].transpose(0, 2, 1),
                           shared(a["L0_ffn_shared_down"].T)])
    arrays = {
        "x": a["L0_attn_x"],
        "w_a": np.concatenate(first + [v2], axis=2),
        "w_b": np.concatenate(second, axis=2),
        "w_o": wo,
        "router": by_chunk(a["L0_ffn_router_weight"]),
        "bias": a["L0_ffn_e_score_correction_bias"],
        "experts": np.concatenate([gate.reshape(EX, P, ND * I), up.reshape(EX, P, ND * I), down],
                                  axis=2),
    }
    arrays = {f"{k}_dram": np.ascontiguousarray(v) for k, v in arrays.items()}
    nc = bacc.Bacc("TRN2", target_bir_lowering=False, num_devices=1)
    args = [nc.dram_tensor(k, v.shape, mybir.dt.from_np(v.dtype), kind="ExternalInput").ap()
            for k, v in arrays.items()]
    out = nc.dram_tensor("out_dram", (B, S, D), F32, kind="ExternalOutput").ap()
    layer(nc, *args, out)
    r = run_bass_kernel_spmd(nc, [arrays], core_ids=[0])
    return r.results[0]["out_dram"]
```

```python
import concourse.bass as bass
import numpy as np
from concourse import mybir
from contextlib import ExitStack

F32 = mybir.dt.float32
F32R = mybir.dt.float32r
BF16 = mybir.dt.bfloat16
ALU = mybir.AluOpType
ACT = mybir.ActivationFunctionType
AX = mybir.AxisListType

P = 128
B, S, D = 2, 1024, 256
H, DH = 16, 128
E, I, SI = 32, 128, 256
G, TOPG, TOPK = 8, 4, 8
SCALE = 2.5
EPS = 1e-5
MASKED = -1.0e30
NEVER = -3.0e38
ND = D // P
NT = S // P
NQ = 512
NC = S // NQ
BC = NQ // P
PAIRS = H // 2
EX = E + SI // I

PAIR = """
T0.0 T0.1 R0.0 X0 T0.2 V0.0 T0.3 V0.1 R0.1 X1 V0.2 V0.3 R0.2 R0.3 W0.0 W0.1 X2 T1.0 T1.1 R1.0
R1.1 X3 T1.2 V1.0 T1.3 R1.2 V1.1 T1.4 V1.2 V1.3 T1.5 R1.3 V1.4 T1.6 T1.7 X4 V1.5 T2.0 V1.6 T2.1
V1.7 X5 T2.2 R2.0 W1.0 R2.1 W1.1 V2.0 V2.1 V2.2 T2.3 X6 V2.3 R2.2 R2.3 W2.0 W2.1 X7 T3.0 T3.1
R3.0 R3.1 X8 V3.0 T3.2 V3.1 T3.3 X9 T3.4 V3.2 T3.5 V3.3 T3.6 V3.4 T3.7 R3.2 V3.5 V3.6 V3.7 X10
R3.3 W3.0 W3.1 X11
"""
START = """
N0.0 N0.1 N0.2 N0.3 N1.0 Y0.0 Y0.1 N1.1 N1.2 N1.3 X4 X5 Y1.0 X8 Y1.1 R3.0 X9 R3.1 X6 R3.2 X7
R3.3 X10 X11
"""
MIDDLE = """
T0.0 T0.1 R0.0 R0.1 V0.0 N2.0 N2.1 X0 T0.2 T0.3 R0.2 R0.3 N3.0 V0.1 N2.2 X1 V0.2 N2.3 T1.0 V0.3
T1.1 X2 R1.0 R1.1 W0.0 W0.1 Y2.0 V1.0 T1.2 R1.2 R1.3 V1.1 N3.1 T1.3 X3 T1.4 V1.2 T1.5 V1.3 N3.2
Y2.1 V1.4 T1.6 T1.7 R2.0 V1.5 N3.3 T2.0 Y3.0 V1.6 T2.1 V1.7 T2.2 Y3.1 R2.1 R2.2 W1.0 X4 R2.3 W1.1
V2.0 T2.3 X5 V2.1 T3.0 V2.2 V2.3 T3.1 X6 W2.0 W2.1 V3.0 V3.1 T3.2 X7 T3.3 R3.0 V3.2 T3.4 X8 V3.3
T3.5 T3.6 R3.1 X9 V3.4 T3.7 R3.2 V3.5 V3.6 V3.7 X10 R3.3 W3.0 W3.1 X11
"""
NEXT_TO_LAST = """
T0.0 T0.1 R0.0 R0.1 N0.0 N0.1 X0 T0.2 R0.2 R0.3 V0.0 V0.1 V0.2 N0.2 T0.3 X1 T1.0 V0.3 N0.3 X2
T1.1 R1.0 N1.0 W0.0 X3 R1.1 W0.1 V1.0 N1.1 X4 T1.2 T1.3 V1.1 Y0.0 R1.2 R1.3 V1.2 N1.2 V1.3 T1.4
T1.5 X5 T1.6 V1.4 T1.7 R2.0 V1.5 V1.6 N1.3 Y0.1 V1.7 T2.0 T2.1 Y1.0 R2.1 W1.0 T2.2 Y1.1 R2.2 R2.3
W1.1 V2.0 T2.3 X6 V2.1 V2.2 T3.0 T3.1 V2.3 L0.0 T3.2 R3.0 W2.0 L0.1 W2.1 V3.0 M0 T3.3 V3.1 G0.0
G0.1 X7 T3.4 R3.1 V3.2 G0.2 T3.5 X8 G0.3 V3.3 T3.6 V3.4 T3.7 X9 R3.2 V3.5 G0.4 V3.6 V3.7 X10 R3.3
W3.0 W3.1 X11
"""
LAST_PAIR = """
R0.0 G0.5 T0.0 T0.1 X0 R0.1 R0.2 G0.6 T0.2 V0.0 T0.3 X1 R0.3 R1.0 G0.7 V0.1 G0.8 X2 V0.2 V0.3
T1.0 T1.1 R1.1 R1.2 W0.0 W0.1 V1.0 R1.3 G0.9 T1.2 T1.3 X3 V1.1 T1.4 V1.2 T1.5 V1.3 T1.6 V1.4
G0.10 T1.7 V1.5 T2.0 V1.6 V1.7 R2.0 R2.1 W1.0 T2.1 R2.2 W1.1 V2.0 T2.2 R2.3 T2.3 V2.1 U0 V2.2
T3.0 V2.3 T3.1 U1 W2.0 W2.1 V3.0 T3.2 V3.1 N2.0 T3.3 T3.4 N2.1 V3.2 T3.5 V3.3 T3.6 V3.4 T3.7 V3.5
N2.2 V3.6 V3.7 N2.3 U2 Y2.0 W3.0 U3 W3.1 N3.0 Y2.1 N3.1 U4 N3.2 N3.3 Z0 D0 Z1 U5 D1 D2 Y3.0 Y3.1
U6 U7 D3 L1.0 U8 L1.1 D4 D5 M1 D6 G1.0 G1.1 D7 U9 G1.2 U10 U11 G1.3 U12 G1.4 G1.5 G1.6 G1.7 D8 D9
D10 U13 G1.8 G1.9 G1.10 D11
"""


def items(order):
    return [(w[0], *(int(i) for i in w[1:].split(".")), *([0] * ("." not in w))) for w in order.split()]


START, PAIR, MIDDLE = items(START), items(PAIR), items(MIDDLE)
NEXT_TO_LAST, LAST_PAIR = items(NEXT_TO_LAST), items(LAST_PAIR)
PROJ = [(1, "q", 0), (1, "k", 0), (1, "q", 1), (1, "k", 1),
        (0, "q", 0), (0, "k", 0), (0, "q", 1), (0, "k", 1)] + [(None, "v", n) for n in range(NT // 2)]
NX = len(PROJ)
X_OWN = 4
ROWS = 2 * NT
TRS = 2 * (BC + NT)
BANKED = TRS + 2 * 2 * NC
NP = B * PAIRS
STATS, APPLY = 2 * BC + 1, BC + 4
UNITS = EX * NC
BODIES = EX // 2
BU = 2 * NC
DONE_BODIES = 3


def flat(t):
    return t[:, :, :].rearrange("p a b -> p (a b)")


def walk(order):
    count = {"TW": 0, "V": 0, "XYLM": 0}
    for kind, k, n in order:
        group = next((g for g in count if kind in g), None)
        yield kind, k, n, count.get(group)
        if group:
            count[group] += 1


def count_of(order, what):
    return next(m for *item, m in walk(order) if tuple(item) == what)


def t_count(k, n):
    return [0, BC, BC + NT, 2 * BC + NT][k] + n


def uses(order):
    return sum(kind in "XYLM" for kind, _, _ in order)


def runs():
    result, x_before = [], uses(START)
    for first, end, order in [(0, PAIRS - 1, PAIR), (PAIRS - 1, PAIRS, MIDDLE), (PAIRS, NP - 2, PAIR),
                              (NP - 2, NP - 1, NEXT_TO_LAST), (NP - 1, NP, LAST_PAIR)]:
        result.append((first, end, order, x_before))
        x_before += (end - first) * uses(order)
    return result


RUNS = runs()


def each_pair(engine, pair):
    for first, end, order, x_before in RUNS:
        b = first // PAIRS
        if end - first == 1:
            pair(b, first, order, x_before)
        else:
            with engine.Fori(first, end) as p:
                pair(b, p, order, (p - first) * NX + x_before)


def norm_of(order, half):
    return half + B * NC if order in (NEXT_TO_LAST, LAST_PAIR) else half


def scored(k):
    return ((k + 1) // 2) % 2, (k + 1) % 2, k == 3


def width(r):
    return P * (r + 1)


def layer(nc, x, w_a, w_b, w_o, router, bias, experts, out):
    with ExitStack() as ctx:
        build(nc, ctx, x, w_a, w_b, w_o, router, bias, experts, out)


def build(nc, ctx, x, w_a, w_b, w_o, router, bias, experts, out):
    def sb(name, shape, dt=F32):
        return ctx.enter_context(nc.sbuf_tensor(name, shape, dt))

    def sem(name):
        return ctx.enter_context(nc.semaphore("s_" + name))

    coeff_dram = [nc.dram_tensor(f"coeff_{b}", [EX, S], F32, kind="Internal").ap() for b in range(B)]

    acc = sb("acc", [P, B * NT, D])
    xT_hi = sb("xT_hi", [P, ND, B * S], F32R)
    xT_lo = sb("xT_lo", [P, ND, B * S], F32R)
    ident, ident_bf = sb("ident", [P, P]), sb("ident_bf", [P, P], BF16)
    causal = sb("causal", [P, P], BF16)
    zero, neg_half = sb("zero", [P, 1]), sb("neg_half", [P, 1])
    xn = sb("xn", [P, NT, D])
    stats, mv = sb("stats", [P, 2, BC, 6]), sb("mv", [P, 2, BC, 2])
    var, inv = sb("var", [P, 2, BC]), sb("inv", [P, 2, BC])
    tmp, tmp2, scale = sb("tmp", [P, 2, BC]), sb("tmp2", [P, 2, BC]), sb("scale", [P, 2, BC])
    raw_a, a_hi, a_lo = sb("raw_a", [P, 1024]), sb("a_hi", [P, 1024], F32R), sb("a_lo", [P, 1024], F32R)
    raw_b, b_hi, b_lo = sb("raw_b", [P, 512]), sb("b_hi", [P, 512], F32R), sb("b_lo", [P, 512], F32R)
    raw_o = sb("raw_o", [P, 2, D])
    o_hi = [sb(f"o_hi{a}", [P, D], F32R) for a in range(2)]
    o_lo = [sb(f"o_lo{a}", [P, D], F32R) for a in range(2)]
    q_hi = [sb(f"q_hi{a}", [P, S], F32R) for a in range(2)]
    q_lo = [sb(f"q_lo{a}", [P, S], F32R) for a in range(2)]
    k_hi = [sb(f"k_hi{a}", [P, S], F32R) for a in range(2)]
    k_lo = [sb(f"k_lo{a}", [P, S], F32R) for a in range(2)]
    v_hi = [sb(f"v_hi{a}", [P, NT, DH], F32R) for a in range(2)]
    v_lo = [sb(f"v_lo{a}", [P, NT, DH], F32R) for a in range(2)]
    v_raw = sb("v_raw", [P, NT, DH])
    prob = [sb(f"prob{c}", [P, BC, NQ * (c + 1)]) for c in range(NC)]
    pT_hi = [sb(f"pT_hi{n}", [P, NQ], F32R) for n in range(3)]
    pT_lo = [sb(f"pT_lo{n}", [P, NQ], F32R) for n in range(3)]
    pL_hi, pL_lo = sb("pL_hi", [P, 2 * P], F32R), sb("pL_lo", [P, 2 * P], F32R)
    z_hi, z_lo = sb("z_hi", [P, NQ], F32R), sb("z_lo", [P, NQ], F32R)
    neg_max = sb("neg_max", [P, NT])
    row_sum, inv_sum = sb("row_sum", [P, NC, BC]), sb("inv_sum", [P, NC, BC])

    rw, bias_bc = sb("router_w", [P, ND, E]), sb("bias_bc", [P, E])
    rw_hi, rw_lo = sb("router_hi", [P, ND, E], F32R), sb("router_lo", [P, ND, E], F32R)
    earlier = sb("earlier", [P, G, G])
    score, biased = sb("score", [P, NT, E]), sb("biased", [P, NT, E])
    pair_a, pair_b, group = sb("pair_a", [P, NT, G]), sb("pair_b", [P, NT, G]), sb("group", [P, NT, G])
    rank, kept = sb("rank", [P, NT, G]), sb("kept", [P, NT, G])
    best, taken = sb("best", [P, NT, 8]), sb("taken", [P, NT, E])
    total, inv_total = sb("total", [P, NT]), sb("inv_total", [P, NT])
    coeff, coT = sb("coeff", [P, NT, E]), sb("coT", [P, NT, E])
    ones = sb("ones", [EX - E, NQ])
    GU = 2 * ND * I
    raw = [sb(f"raw{n}", [P, GU + D]) for n in range(2)]
    gu_hi = [sb(f"gu_hi{n}", [P, GU], F32R) for n in range(2)]
    gu_lo = [sb(f"gu_lo{n}", [P, GU], F32R) for n in range(2)]
    dn_hi = [sb(f"dn_hi{n}", [P, D], F32R) for n in range(2)]
    dn_lo = [sb(f"dn_lo{n}", [P, D], F32R) for n in range(2)]
    h = [sb(f"h{n}", [P, NQ]) for n in range(2)]
    rank_parts = [[t.rearrange("p (t g h) -> p t g h", g=G, h=G) for t in parts]
                  for parts in ([h[0][:, :], h[1][:, :]], [raw_b[:, :], flat(raw_o)])]
    co = [prob[0][:, 2 * n:2 * n + 2, :].rearrange("p a b -> p (a b)") for n in range(2)]
    oT = prob[1][:, 0:ND, :]
    sg = [raw_a[:, n * NQ:(n + 1) * NQ] for n in range(2)]
    gated = [flat(v_raw)[:, n * NQ:(n + 1) * NQ] for n in range(2)]
    HB = 4
    h_hi = [q_hi[n // 2][:, n % 2 * NQ:(n % 2 + 1) * NQ] for n in range(HB)]
    h_lo = [q_lo[n // 2][:, n % 2 * NQ:(n % 2 + 1) * NQ] for n in range(HB)]
    zeros = pL_hi[:, 0:P]

    expT = xn[0:E, 0:S // D, :].rearrange("p t d -> p (t d)")

    ps_s = [ctx.enter_context(nc.psum_tensor(f"ps_s{n}", [P, S], F32)) for n in range(2)]
    ps_t = [ctx.enter_context(nc.psum_tensor(f"ps_t{n}", [P, NQ], F32)) for n in range(2)]
    ps_z = ctx.enter_context(nc.psum_tensor("ps_z", [P, NQ], F32))
    ps_x = ctx.enter_context(nc.psum_tensor("ps_x", [P, NQ], F32))
    ps_gu = [[ps_s[c][:, m * NQ:(m + 1) * NQ] for m in range(2)] for c in range(NC)]
    ps_o = [[ps_t[0][:, :], ps_t[1][:, :]], [ps_z[:, :], ps_x[:, :]]]

    def in_gu(order, kind, k):
        return order is LAST_PAIR and (kind, k) in (("Y", B * NC - 1), ("L", B - 1), ("M", B - 1))

    def bank_of(order, kind, k, n):
        return ps_gu[NC - 1][n] if in_gu(order, kind, k) else ps_x[:, :]

    s_const, s_load = sem("const"), [sem(f"load{n}") for n in range(B * NT // 2)]
    s_ones, s_in, s_router = sem("ones"), sem("in"), sem("router")
    s_raw_a, s_raw_b = sem("raw_a"), sem("raw_b")
    s_raw_o = [sem(f"raw_o{a}") for a in range(2)]
    s_stats, s_pow, s_apply = sem("stats"), sem("pow"), sem("apply")
    s_a, s_b, s_v1 = sem("split_a"), sem("split_b"), sem("split_v1")
    s_o = [sem(f"split_o{a}") for a in range(2)]
    s_pool = sem("pool_hi")
    s_scores, s_max, s_exp = sem("scores"), sem("max"), sem("exp")
    s_bank, s_hi, s_bank_free = sem("bank"), sem("pT_hi"), sem("bank_free")
    s_pv = sem("pv")
    s_x, s_x_hi, s_x_free = sem("x"), sem("x_hi"), sem("x_free")
    s_z_hi, s_z_lo = sem("z_hi"), sem("z_lo")
    s_inv = sem("inv_sum")
    s_route, s_coT, s_co_dram = sem("route"), sem("coT"), sem("co_dram")
    s_raw = [sem(f"raw{n}") for n in range(2)]
    s_co_in = [sem(f"co_in{n}") for n in range(2)]
    s_gu, s_silu, s_gu_free = sem("gu"), sem("silu"), sem("gu_free")
    s_h, s_h_hi, s_h_lo, s_dn = sem("h"), sem("h_hi"), sem("h_lo"), sem("dn")
    s_gu_w, s_dn_w = sem("gu_w"), sem("dn_w")
    s_oT_act, s_oT_dve, s_oT_ps = sem("oT_act"), sem("oT_dve"), sem("oT_ps")
    s_final, s_out = sem("final"), [sem(f"out{b}") for b in range(B)]
    EXP0, BANK0, PV0, X0, O0 = 2, 2, 3, 1, 1
    GU0, DN0, GUF0, W0, H0 = 4, 4, 2, 2, 2 * NC
    CONSTS = 12
    X_SCORES = [X0 + RUNS[b - B][3] + count_of(RUNS[b - B][2], ("M", b, 0)) + 1 for b in range(B)]

    def store_out(engine, n):
        b, t = divmod(2 * n, NT)
        engine.wait_ge(s_final, n + 1)
        engine.dma_start(out[b, t * P:(t + 2) * P, :].rearrange("(t p) d -> p t d", p=P),
                         acc[:, 2 * n:2 * n + 2, :]).then_inc(s_out[b], 16)

    block = ctx.enter_context(nc.Block())

    @block.sync
    def _(sp):
        for n in range(B * NT // 2):
            b, t = divmod(2 * n, NT)
            sp.dma_start(acc[:, 2 * n:2 * n + 2, :],
                         x[b, t * P:(t + 2) * P, :].rearrange("(t p) d -> p t d", p=P))\
                .then_inc(s_load[n], 16)
        sp.dma_start(rw[:, :, :], router).then_inc(s_in, 16)
        sp.dma_start(bias_bc[:, :], bias.partition_broadcast(P)).then_inc(s_in, 16)
        sp.wait_ge(s_ones, 1)
        for b in range(B):
            for c in range(NC):
                sp.dma_start(coeff_dram[b][E:EX, c * NQ:(c + 1) * NQ], ones[:, 0:NQ])\
                    .then_inc(s_co_dram, 16)
        stored = 16 * B * NC

        def pair(p, now, then):
            sp.wait_ge(s_a, 2 * (p + 1))
            if then is not None:
                sp.dma_start(raw_a[:, :], w_a[then]).then_inc(s_raw_a, 16)
            sp.wait_ge(s_o[1], p + O0)
            sp.dma_start(raw_o[:, 1, :], w_o[now * 2 + 1]).then_inc(s_raw_o[1], 16)
            sp.wait_ge(s_b, p + 1)
            if then is not None:
                sp.dma_start(raw_b[:, :], w_b[then]).then_inc(s_raw_b, 16)
            sp.wait_ge(s_o[0], p + 1)
            if then is not None:
                sp.dma_start(raw_o[:, 0, :], w_o[then * 2]).then_inc(s_raw_o[0], 16)

        for b in range(B):
            with sp.Fori(0, PAIRS - 1) as i:
                pair(b * PAIRS + i, i, i + 1)
            pair(b * PAIRS + PAIRS - 1, PAIRS - 1, 0 if b == 0 else None)

        def store(b):
            nonlocal stored
            sp.wait_ge(s_coT, b + 1)
            to = coeff_dram[b][0:E, :].rearrange("e (t q r) -> q e t r", q=4, r=E)
            for q in range(4):
                sp.dma_start(to[q], coT[q * E:(q + 1) * E, :, :]).then_inc(s_co_dram, 16)
            stored += 16 * 4
            sp.wait_ge(s_co_dram, stored)

        def load_weights(b, i, n):
            sp.wait_ge(s_dn_w, b * EX + i * 2 + n - 1 + W0)
            sp.dma_start(raw[n][:, :], experts[i * 2 + n]).then_inc(s_raw[n], 16)

        def load_coefficients(b, i, n):
            sp.wait_ge(s_h, (b * EX + i * 2 + n - 1) * NC + H0)
            sp.dma_start(co[n], coeff_dram[b][i * 2 + n].partition_broadcast(P))\
                .then_inc(s_co_in[n], 16)

        def loads(b, i):
            for n in range(2):
                load_weights(b, i, n)
                load_coefficients(b, i, n)

        for i in range(2):
            for n in range(2):
                load_weights(0, i, n)
        store(0)
        sp.wait_ge(s_bank, (NP - 1) * BANKED + count_of(LAST_PAIR, ("T", 2, BC - 1)) + 1)
        for i in range(2):
            for n in range(2):
                load_coefficients(0, i, n)
        with sp.Fori(2, 6) as i:
            loads(0, i)
        store(1)
        with sp.Fori(6, BODIES) as i:
            loads(0, i)
        with sp.Fori(0, 2) as i:
            loads(1, i)
        for n in range(2 * NC):
            store_out(sp, n)
        with sp.Fori(2, BODIES) as i:
            loads(1, i)

    @block.gpsimd
    def _(pool):
        pool.memset(ident[:, :], 0.0).then_inc(s_const, 1)
        pool.memset(neg_half[:, :], -0.5).then_inc(s_const, 1)
        pool.memset(zero[:, :], 0.0).then_inc(s_const, 1)
        pool.memset(ident_bf[:, :], 0.0).then_inc(s_const, 1)
        pool.memset(causal[:, :], 0.0).then_inc(s_const, 1)
        pool.wait_ge(s_const, 5)
        for m in (ident, ident_bf):
            pool.affine_select(out=m[:, :], in_=m[:, :], compare_op=ALU.not_equal, fill=1.0,
                               base=0, pattern=[[-1, P]], channel_multiplier=1).then_inc(s_const, 1)
        pool.affine_select(out=causal[:, :], in_=causal[:, :], compare_op=ALU.is_ge, fill=MASKED,
                           base=0, pattern=[[-1, P]], channel_multiplier=1).then_inc(s_const, 1)

        pool.sem_inc(s_o[1], O0)
        pool.sem_inc(s_gu_w, W0)
        pool.sem_inc(s_dn_w, W0)

        def split(hi, lo, src, count, done):
            pool.tensor_tensor(hi, src, zero[:, 0:1].to_broadcast([P, src.shape[-1]]),
                               ALU.add).then_inc(s_pool, 1)
            pool.wait_ge(s_pool, count + 1)
            pool.tensor_tensor(lo, src, hi.bitcast(F32), ALU.subtract).then_inc(done, 1)

        def power(q):
            pool.wait_ge(s_stats, (q + 1) * STATS)
            pool.tensor_tensor(inv[:, q % 2, :], var[:, q % 2, :],
                               neg_half[:, 0:1].to_broadcast([P, BC]), ALU.pow).then_inc(s_pow, 1)

        def split_a(count):
            for part in range(2):
                at = slice(part * 512, (part + 1) * 512)
                split(a_hi[:, at], a_lo[:, at], raw_a[:, at], count + part, s_a)

        power(0)
        pool.wait_ge(s_raw_a, 16)
        split_a(0)
        power(1)
        pool.wait_ge(s_raw_b, 16)
        split(b_hi[:, :], b_lo[:, :], raw_b[:, :], 2, s_b)
        pool.wait_ge(s_raw_o[0], 16)
        split(o_hi[0][:, :], o_lo[0][:, :], raw_o[:, 0, :], 3, s_o[0])
        pool.wait_ge(s_in, 32)
        split(flat(rw_hi), flat(rw_lo), flat(rw), 4, s_router)
        pool.memset(pL_hi[:, 0:P].bitcast(F32), 0.0).then_inc(s_const, 1)
        pool.memset(pL_lo[:, 0:P].bitcast(F32), 0.0).then_inc(s_const, 1)
        pool.memset(ones[:, 0:NQ], 1.0).then_inc(s_ones, 1)
        pool.memset(earlier[:, :, :], 1.0).then_inc(s_const, 1)
        pool.wait_ge(s_const, 11)
        pool.affine_select(out=earlier[:, :, :], in_=earlier[:, :, :], compare_op=ALU.is_gt, fill=0.0,
                           base=0, pattern=[[1, G], [-1, G]], channel_multiplier=0).then_inc(s_const, 1)

        def split_v1(p, count, x_before):
            pool.wait_ge(s_x_free, x_before + X0)
            pool.wait_ge(s_pv, PV0 + p * TRS)
            split(flat(v_hi[1]), flat(v_lo[1]), flat(v_raw), count, s_v1)

        def split_o1(p, count):
            pool.wait_ge(s_raw_o[1], 16 * p + 16)
            pool.wait_ge(s_bank, p * BANKED + 1)
            split(o_hi[1][:, :], o_lo[1][:, :], raw_o[:, 1, :], count, s_o[1])

        def pair(_, p, order, x_before):
            n = 6 * p + 5
            if order is not LAST_PAIR:
                pool.wait_ge(s_raw_a, 16 * p + 32)
                pool.wait_ge(s_x, x_before)
                split_a(n)
                n += 2
                if order is MIDDLE:
                    power(2)
                    power(3)
                elif order is NEXT_TO_LAST:
                    power(4)
                    power(5)
            split_v1(p, n, x_before)
            split_o1(p, n + 1)
            if order is LAST_PAIR:
                return
            pool.wait_ge(s_raw_b, 16 * p + 32)
            pool.wait_ge(s_x, x_before + count_of(order, ("X", X_OWN - 1, 0)) + 1)
            split(b_hi[:, :], b_lo[:, :], raw_b[:, :], n + 2, s_b)
            pool.wait_ge(s_raw_o[0], 16 * p + 32)
            pool.wait_ge(s_pv, PV0 + p * TRS + t_count(2, 0) + 1)
            split(o_hi[0][:, :], o_lo[0][:, :], raw_o[:, 0, :], n + 3, s_o[0])

        each_pair(pool, pair)
        before = 6 * (NP - 1) + 7

        def gate_up(e, n, nth, count):
            pool.wait_ge(s_raw[n], 16 * nth + 16)
            pool.wait_ge(s_gu, (e - 1) * NC + GU0)
            split(gu_hi[n][:, :], gu_lo[n][:, :], raw[n][:, 0:GU], before + count, s_gu_w)

        def down(e, n, count):
            pool.wait_ge(s_dn, (e - 1) * NC + DN0)
            split(dn_hi[n][:, :], dn_lo[n][:, :], raw[n][:, GU:], before + count, s_dn_w)

        gate_up(0, 0, 0, 0)
        gate_up(1, 1, 0, 1)
        down(0, 0, 2)
        down(1, 1, 3)
        power(6)
        gate_up(2, 0, 1, 4)
        gate_up(3, 1, 1, 5)
        power(7)
        down(2, 0, 6)
        with pool.Fori(2, B * BODIES) as i:
            for n in range(2):
                e = i * 2 + n
                gate_up(e, n, i, 2 * e - 1)
                down(e - 1, 1 - n, 2 * e)
        down(B * EX - 1, 1, 2 * B * EX - 1)

    @block.tensor
    def _(pe):
        pe.sem_inc(s_pv, PV0)
        pe.sem_inc(s_gu, GU0)
        pe.sem_inc(s_dn, DN0)
        pe.wait_ge(s_const, 8)

        def three(to, w_hi, w_lo, m_hi, m_lo, start, stop):
            pe.matmul(to, w_hi, m_hi, start=start, stop=False)
            pe.matmul(to, w_hi, m_lo, start=False, stop=False)
            return pe.matmul(to, w_lo, m_hi, start=False, stop=stop)

        def transpose_xn(q, d, bank):
            for t in range(BC):
                pe.wait_ge(s_apply, (q + 1) * APPLY - BC + t + 1)
                last = pe.transpose(bank[:, t * P:(t + 1) * P],
                                    xn[:, q % NC * BC + t, d * P:(d + 1) * P], ident[:, :])
            last.then_inc(s_x, 1)

        def project(b, n, bank, weights):
            a, what, part = PROJ[n]
            if a == 1:
                pe.wait_ge(s_b, weights)
                w_hi, w_lo = b_hi, b_lo
            else:
                pe.wait_ge(s_a, weights)
                w_hi, w_lo = a_hi, a_lo
            if what == "v":
                for j in range(2):
                    t = b * S + (2 * part + j) * P
                    for d in range(ND):
                        m = slice(512 + d * 2 * DH, 512 + (d + 1) * 2 * DH)
                        last = three(bank[:, j * 2 * DH:(j + 1) * 2 * DH],
                                     xT_hi[:, d, t:t + P], xT_lo[:, d, t:t + P],
                                     w_hi[:, m], w_lo[:, m], d == 0, d == ND - 1)
            else:
                at = 0 if what == "q" else ND * DH
                t = b * S + part * NQ
                for d in range(ND):
                    w = slice(at + d * DH, at + (d + 1) * DH)
                    last = three(bank[:, :], w_hi[:, w], w_lo[:, w], xT_hi[:, d, t:t + NQ],
                                 xT_lo[:, d, t:t + NQ], d == 0, d == ND - 1)
            last.then_inc(s_x, 1)

        def scores(a, r, row, x_need):
            pe.wait_ge(s_exp, row + EXP0 - 1)
            pe.wait_ge(s_x_free, x_need + X0)
            q = slice(r * P, (r + 1) * P)
            to = ps_s[r % 2]
            for k0 in range(0, width(r), NQ):
                k1 = max(min(width(r), k0 + NQ), k0 + 2 * P)
                diagonal = k0 <= r * P < k1
                last = three(to[:, k0:k1], q_hi[a][:, q], q_lo[a][:, q], k_hi[a][:, k0:k1],
                             k_lo[a][:, k0:k1], True, not diagonal)
                if diagonal:
                    last = pe.matmul(to[:, r * P:(r + 1) * P], ident_bf[:, :], causal[:, :],
                                     start=False, stop=True)
            last.then_inc(s_scores, 1)

        def transpose(c, n, bank, use, rows):
            pe.wait_ge(s_bank_free, use + BANK0 - 1)
            pe.wait_ge(s_exp, rows + EXP0)
            for j in range(max(n - c * BC, 0), BC):
                last = pe.transpose(bank[:, j * P:(j + 1) * P], prob[c][:, j, n * P:(n + 1) * P],
                                    ident[:, :])
            last.then_inc(s_bank, 1)

        def times_v(a, c, n, t, t_use):
            pe.wait_ge(s_bank_free, t_use + BANK0 + 1)
            diag = max(n - c * BC, 0)
            if diag == BC - 1:
                m_hi, m_lo, q0 = pL_hi[:, :], pL_lo[:, :], (BC - 2) * P
            else:
                q0 = diag * P
                m_hi, m_lo = pT_hi[t % 3][:, q0:], pT_lo[t % 3][:, q0:]
            three(ps_z[:, q0:], v_hi[a][:, n, :], v_lo[a][:, n, :], m_hi, m_lo, n == 0,
                  n == (c + 1) * BC - 1).then_inc(s_pv, 1)

        def project_out(a, n, bank, use, chunk, weights):
            pe.wait_ge(s_bank_free, use + BANK0 - 1)
            pe.wait_ge(s_z_lo, chunk)
            pe.wait_ge(s_o[a], weights)
            for j in range(2):
                q = slice((2 * n + j) * P, (2 * n + j + 1) * P)
                last = three(bank[:, j * D:(j + 1) * D], z_hi[:, q], z_lo[:, q],
                             o_hi[a][:, :], o_lo[a][:, :], True, True)
            last.then_inc(s_bank, 1)

        def attend(kind, k, n, m, p, order, x_before):
            a, c = k // 2, k % 2
            if kind == "R":
                na, c_, is_next = scored(k)
                r = c_ * BC + n
                scores(na, r, (p + 1) * ROWS + r if is_next else p * ROWS + na * NT + r,
                       x_before - 2 if k == 0 else
                       x_before + count_of(order, ("X", 2 * k - 1, 0)) + 1)
            elif kind == "T":
                transpose(c, n, ps_t[m % 2], p * BANKED + m, p * ROWS + a * NT + (c + 1) * BC)
            elif kind == "V":
                if a == 1 and n == 0:
                    pe.wait_ge(s_v1, p + 1)
                times_v(a, c, n, m, p * BANKED + count_of(order, ("T", k, n)))
            elif kind == "W":
                project_out(a, n, ps_t[m % 2], p * BANKED + m, p * 4 + k + 1,
                            p + 1 if a == 0 else p + 1 + O0)

        def logits(b, c, to):
            at = slice(b * S + c * NQ, b * S + (c + 1) * NQ)
            for d in range(ND):
                last = three(to[0:E, :], rw_hi[:, d, :], rw_lo[:, d, :], xT_hi[:, d, at],
                             xT_lo[:, d, at], d == 0, d == ND - 1)
            last.then_inc(s_x, 1)

        def transpose_scores(to):
            for t in range(NT):
                last = pe.transpose(to[:, t * E:(t + 1) * E], expT[:, t * P:(t + 1) * P],
                                    ident[0:E, 0:E])
            last.then_inc(s_x, 1)

        def gate_up(b, slot, u, e):
            n, c = slot // NC, slot % NC
            pe.wait_ge(s_gu_free, u + GUF0 - 1)
            pe.wait_ge(s_gu_w, e + 1 + W0)
            at = slice(b * S + c * NQ, b * S + (c + 1) * NQ)
            for m in range(2):
                for d in range(ND):
                    w = slice((m * ND + d) * I, (m * ND + d + 1) * I)
                    last = three(ps_gu[c][m], gu_hi[n][:, w], gu_lo[n][:, w],
                                 xT_hi[:, d, at], xT_lo[:, d, at], d == 0, d == ND - 1)
            last.then_inc(s_gu, 1)

        def down(slot, u, e, stop):
            n, c = slot // NC, slot % NC
            pe.wait_ge(s_h_lo, u + 1)
            pe.wait_ge(s_dn_w, e + 1 + W0)
            for d in range(ND):
                w = slice(d * P, (d + 1) * P)
                last = three(ps_o[c][d], dn_hi[n][:, w], dn_lo[n][:, w], h_hi[slot], h_lo[slot],
                             False, stop)
            last.then_inc(s_dn, 1)

        def clear(c):
            for d in range(ND):
                pe.matmul(ps_o[c][d], zeros, xT_hi[:, d, 0:NQ], start=True, stop=False)

        for kind, k, n, m in walk(START):
            bank = [ps_x, ps_z][(m or 0) % 2]
            if kind in "XY" and m >= 2:
                pe.wait_ge(s_x_free, X0 + m - 1)
            if kind == "Y":
                transpose_xn(k, n, bank)
            elif kind == "X":
                half = 1 if PROJ[k][1] != "v" and PROJ[k][2] == 1 or k >= X_OWN + 6 else 0
                pe.wait_ge(s_x_free, X0 + count_of(START, ("Y", half, ND - 1)) + 1)
                project(0, k, bank, 1 if k < X_OWN + 4 else 2)
            elif kind == "R":
                scores(0, n, n, count_of(START, ("X", X_OWN + 1, 0)) + 1)
        pe.wait_ge(s_const, CONSTS)
        pe.wait_ge(s_router, 1)

        def pair(b, p, order, x_before):
            then = 1 if order is MIDDLE else b
            ps_x_used = borrowed = units = 0
            for kind, k, n, m in walk(order):
                if kind in "XYLM":
                    pe.wait_ge(s_x_free, x_before + m + X0)
                    if in_gu(order, kind, k):
                        pe.wait_ge(s_gu_free, GUF0 + units // NC * NC)
                        borrowed = m + 1
                    else:
                        ps_x_used = m + 1
                if kind == "X":
                    own = k < X_OWN
                    project(b if own else then, k, ps_x,
                            p + 1 if own else 2 * (p + 1) + (1 if k < X_OWN + 4 else 2))
                elif kind == "Y":
                    transpose_xn(norm_of(order, k), n, bank_of(order, kind, k, n))
                elif kind == "L":
                    logits(k, n, bank_of(order, kind, k, n))
                elif kind == "M":
                    transpose_scores(bank_of(order, kind, k, n))
                elif kind == "U":
                    if k < NC:
                        pe.wait_ge(s_exp, NP * ROWS + EXP0 - NC + 1 + k)
                    elif k % NC and borrowed:
                        pe.wait_ge(s_x_free, x_before + borrowed + X0)
                    gate_up(0, k % HB, k, k // NC)
                    units += 1
                elif kind == "Z":
                    if k == 0:
                        pe.wait_ge(s_bank_free, BANK0 + NP * BANKED)
                    else:
                        pe.wait_ge(s_x_free, x_before + ps_x_used + X0)
                    clear(k)
                elif kind == "D":
                    down(k % HB, k, k // NC, False)
                else:
                    attend(kind, k, n, m, p, order, x_before)

        each_pair(pe, pair)

        def body(b, i):
            for j in range(BU):
                u = b * UNITS + i * BU + j
                f = j + NC
                gate_up(b, f % HB, u + NC, b * EX + i * 2 + f // NC)
                down(j, u, b * EX + i * 2 + j // NC, False)

        def last_body(b):
            for j in range(BU):
                u = (b + 1) * UNITS - BU + j
                f = j + NC
                if f < BU:
                    gate_up(b, f, u + NC, (b + 1) * EX - 1)
                elif b + 1 < B:
                    gate_up(b + 1, f % HB, u + NC, (b + 1) * EX)
                down(j, u, (b + 1) * EX - 2 + j // NC, j >= NC)

        def transpose_out(b, c):
            pe.wait_ge(s_oT_act, b * NC + c + 1)
            pe.wait_ge(s_oT_dve, b * NC + c + 1)
            for half in range(2):
                for t in range(2):
                    for d in range(ND):
                        q = c * NQ + (half * 2 + t) * P
                        last = pe.transpose(ps_o[c][half][:, t * D + d * P:t * D + (d + 1) * P],
                                            oT[:, d, q:q + P], ident[:, :])
                last.then_inc(s_oT_ps, 1)

        with pe.Fori(DONE_BODIES, BODIES - 1) as i:
            body(0, i)
        last_body(0)
        first = UNITS
        transpose_out(0, 0)
        gate_up(1, 2, first + 2, EX + 1)
        transpose_out(0, 1)
        for c in range(NC):
            pe.wait_ge(s_final, 2 * (c + 1))
            clear(c)
            down(c, first + c, EX, False)
            gate_up(1, (c + 3) % HB, first + c + 3, EX + (c + 3) // NC)
        down(2, first + 2, EX + 1, False)
        gate_up(1, 1, first + 5, EX + 2)
        down(3, first + 3, EX + 1, False)
        with pe.Fori(1, BODIES - 1) as i:
            body(1, i)
        last_body(1)
        for c in range(NC):
            transpose_out(1, c)

    @block.scalar
    def _(act):
        act.dma_start(raw_a[:, :], w_a[0]).then_inc(s_raw_a, 16)
        act.dma_start(raw_b[:, :], w_b[0]).then_inc(s_raw_b, 16)
        act.dma_start(raw_o[:, 0, :], w_o[0]).then_inc(s_raw_o[0], 16)
        act.sem_inc(s_exp, EXP0)

        def xn_high(half, d, bank, use):
            act.wait_ge(s_x, use + 1)
            act.activation(xT_hi[:, d, half * NQ:(half + 1) * NQ], bank[:, :],
                           ACT.Copy).then_inc(s_x_hi, 1)

        def project(n, bank, use):
            a, what, part = PROJ[n]
            act.wait_ge(s_x, use + 1)
            if what == "v":
                src = bank[:, :].rearrange("p (t a h) -> p a t h", t=2, a=2)
                t = slice(2 * part, 2 * part + 2)
                act.activation(v_raw[:, t, :], src[:, 1], ACT.Copy)
                act.activation(v_hi[0][:, t, :], src[:, 0], ACT.Copy).then_inc(s_x_hi, 1)
            elif what == "q":
                act.activation(q_hi[a][:, part * NQ:(part + 1) * NQ], bank[:, :], ACT.Copy,
                               scale=DH ** -0.5).then_inc(s_x_hi, 1)
            else:
                act.activation(k_hi[a][:, part * NQ:(part + 1) * NQ], bank[:, :],
                               ACT.Copy).then_inc(s_x_hi, 1)

        def exponentials(r, row):
            act.wait_ge(s_max, row + 1)
            c, j = r // BC, r % BC
            act.activation(prob[c][:, j, 0:width(r)], ps_s[r % 2][:, 0:width(r)], ACT.Exp,
                           bias=neg_max[:, r:r + 1],
                           accum_out=row_sum[:, c, j:j + 1]).then_inc(s_exp, 1)

        def attend(kind, k, n, m, p):
            c = k % 2
            if kind == "R":
                na, c_, is_next = scored(k)
                r = c_ * BC + n
                exponentials(r, (p + 1) * ROWS + r if is_next else p * ROWS + na * NT + r)
            elif kind == "T":
                t = t_count(k, n)
                act.wait_ge(s_bank, p * BANKED + m + 1)
                act.wait_ge(s_pv, p * TRS + t + PV0 - 2)
                j = max(n - c * BC, 0)
                to = pL_hi[:, P:] if j == BC - 1 else pT_hi[t % 3][:, j * P:]
                act.activation(to, ps_t[m % 2][:, j * P:], ACT.Copy).then_inc(s_hi, 1)
            elif kind == "V" and n == (c + 1) * BC - 1:
                act.wait_ge(s_pv, p * TRS + m + PV0 + 1)
                act.activation(z_hi[:, :], ps_z[:, :], ACT.Copy).then_inc(s_z_hi, 1)

        def high(slot, u):
            act.wait_ge(s_h, u + 1 + H0)
            act.wait_ge(s_dn, u + 1)
            act.activation(h_hi[slot], h[slot % 2][:, :], ACT.Copy).then_inc(s_h_hi, 1)

        def unit(slot, u, first=False):
            act.wait_ge(s_gu, u + 1 + GU0)
            act.activation(sg[slot % 2], ps_gu[slot % 2][0], ACT.Silu).then_inc(s_silu, 1)
            if not first:
                high((slot - 1) % HB, u - 1)

        for kind, k, n, m in walk(START):
            bank = [ps_x, ps_z][(m or 0) % 2]
            if kind == "Y":
                xn_high(k, n, bank, m)
            elif kind == "X":
                project(k, bank, m)
            elif kind == "R":
                exponentials(n, n)

        def pair(_, p, order, x_before):
            for kind, k, n, m in walk(order):
                if kind == "X":
                    project(k, ps_x, x_before + m)
                elif kind == "Y":
                    xn_high(k, n, bank_of(order, kind, k, n), x_before + m)
                elif kind == "L":
                    act.wait_ge(s_x, x_before + m + 1)
                    act.activation(expT[:, n * NQ:(n + 1) * NQ],
                                   bank_of(order, kind, k, n)[0:E, :], ACT.Exp,
                                   scale=-1.0).then_inc(s_x_hi, 1)
                elif kind == "M":
                    act.wait_ge(s_x, x_before + m + 1)
                    act.activation(flat(score), bank_of(order, kind, k, n)[:, 0:NT * E],
                                   ACT.Copy).then_inc(s_x_hi, 1)
                elif kind == "U":
                    unit(k % HB, k, k == 0)
                else:
                    attend(kind, k, n, m, p)

        each_pair(act, pair)

        def copy_out(b, c):
            act.wait_ge(s_dn, (b + 1) * UNITS - NC + c + 1 + DN0)
            act.activation(oT[:, 0, c * NQ:(c + 1) * NQ], ps_o[c][0], ACT.Copy).then_inc(s_oT_act, 1)

        def body(b, i):
            for j in range(BU):
                unit((j + NC) % HB, b * UNITS + i * BU + j + NC)

        with act.Fori(DONE_BODIES, BODIES - 1) as i:
            body(0, i)
        last = UNITS - NC
        for j in range(NC):
            unit(j + NC, last + j)
        for c in range(NC):
            unit(c, UNITS + c)
            copy_out(0, c)
        with act.Fori(0, BODIES - 1) as i:
            body(1, i)
        for j in range(NC):
            unit(j + NC, UNITS + last + j, j > 0)
            high(j + NC, UNITS + last + j)
        for c in range(NC):
            copy_out(1, c)
        for n in range(2 * NC, 2 * B * NC):
            store_out(act, n)
        for b in range(B):
            act.wait_ge(s_out[b], 16 * 2 * NC)

    @block.vector
    def _(dve):
        dve.sem_inc(s_bank_free, BANK0)
        dve.sem_inc(s_x_free, X0)
        dve.sem_inc(s_gu_free, GUF0)
        dve.sem_inc(s_h, H0)

        def norm(q, stage):
            k, tile = q % 2, q % (B * NC) * BC
            if stage < 2 and q < B * NC:
                dve.wait_ge(s_load[2 * q + stage], 16)
            if stage < 2:
                own = q * STATS
                for t in range(2 * stage, 2 * stage + 2):
                    dve.bn_stats(stats[:, k, t, :], acc[:, tile + t, :]).then_inc(s_stats, 1)
                if stage == 1:
                    dve.wait_ge(s_stats, own + BC)
                    for t in range(BC):
                        dve.bn_aggr(mv[:, k, t, :], stats[:, k, t, :]).then_inc(s_stats, 1)
                    dve.wait_ge(s_stats, own + 2 * BC)
                    dve.tensor_scalar(var[:, k, :], mv[:, k, :, 1], EPS, None,
                                      ALU.add).then_inc(s_stats, 1)
                return
            if stage == 2:
                own = q * APPLY
                dve.wait_ge(s_pow, q + 1)
                dve.tensor_tensor(tmp[:, k, :], inv[:, k, :], inv[:, k, :],
                                  ALU.mult).then_inc(s_apply, 1)
                dve.wait_ge(s_apply, own + 1)
                dve.tensor_tensor(tmp2[:, k, :], tmp[:, k, :], var[:, k, :],
                                  ALU.mult).then_inc(s_apply, 1)
                dve.wait_ge(s_apply, own + 2)
                dve.tensor_scalar(tmp[:, k, :], tmp2[:, k, :], -0.5, 1.5, ALU.mult, ALU.add)\
                    .then_inc(s_apply, 1)
                dve.wait_ge(s_apply, own + 3)
                dve.tensor_tensor(scale[:, k, :], inv[:, k, :], tmp[:, k, :],
                                  ALU.mult).then_inc(s_apply, 1)
                dve.wait_ge(s_apply, own + 4)
            for t in range(2 * stage - 4, 2 * stage - 2):
                dve.tensor_scalar(xn[:, q % NC * BC + t, :], acc[:, tile + t, :], mv[:, k, t, 0:1],
                                  scale[:, k, t:t + 1], ALU.subtract, ALU.mult).then_inc(s_apply, 1)

        def xn_low(half, d, bank, use):
            at = slice(half * NQ, (half + 1) * NQ)
            dve.wait_ge(s_x_hi, use + 1)
            dve.tensor_tensor(xT_lo[:, d, at], bank[:, :], xT_hi[:, d, at].bitcast(F32),
                              ALU.subtract).then_inc(s_x_free, 1)

        def project(n, bank, use):
            a, what, part = PROJ[n]
            dve.wait_ge(s_x_hi, use + 1)
            if what == "v":
                src = bank[:, :].rearrange("p (t a h) -> p a t h", t=2, a=2)
                t = slice(2 * part, 2 * part + 2)
                dve.tensor_tensor(v_lo[0][:, t, :], src[:, 0], v_hi[0][:, t, :].bitcast(F32),
                                  ALU.subtract).then_inc(s_x_free, 1)
            elif what == "q":
                at = slice(part * NQ, (part + 1) * NQ)
                dve.scalar_tensor_tensor(q_lo[a][:, at], bank[:, :], DH ** -0.5,
                                         q_hi[a][:, at].bitcast(F32), ALU.mult,
                                         ALU.subtract).then_inc(s_x_free, 1)
            else:
                at = slice(part * NQ, (part + 1) * NQ)
                dve.tensor_tensor(k_lo[a][:, at], bank[:, :], k_hi[a][:, at].bitcast(F32),
                                  ALU.subtract).then_inc(s_x_free, 1)

        def maximum(r, row):
            dve.wait_ge(s_scores, row + 1)
            dve.tensor_reduce(neg_max[:, r:r + 1], ps_s[r % 2][:, 0:width(r)], AX.X, ALU.max,
                              negate=True).then_inc(s_max, 1)

        def attend(kind, k, n, m, b, p):
            a, c = k // 2, k % 2
            if kind == "R":
                na, c_, is_next = scored(k)
                r = c_ * BC + n
                maximum(r, (p + 1) * ROWS + r if is_next else p * ROWS + na * NT + r)
            elif kind == "T":
                t = t_count(k, n)
                j = max(n - c * BC, 0)
                hi = pL_hi[:, P:] if j == BC - 1 else pT_hi[t % 3][:, j * P:]
                lo = pL_lo[:, P:] if j == BC - 1 else pT_lo[t % 3][:, j * P:]
                dve.wait_ge(s_hi, p * TRS + t + 1)
                dve.tensor_tensor(lo, ps_t[m % 2][:, j * P:], hi.bitcast(F32),
                                  ALU.subtract).then_inc(s_bank_free, 1)
                if n == 0:
                    dve.reciprocal(inv_sum[:, c, :], row_sum[:, c, :]).then_inc(s_inv, 1)
            elif kind == "V" and n == (c + 1) * BC - 1:
                dve.wait_ge(s_z_hi, p * 4 + k + 1)
                dve.tensor_tensor(z_lo[:, :], ps_z[:, :], z_hi[:, :].bitcast(F32),
                                  ALU.subtract).then_inc(s_z_lo, 1)
            elif kind == "W":
                dve.wait_ge(s_bank, p * BANKED + m + 1)
                dve.wait_ge(s_inv, p * 4 + k + 1)
                for j in range(2):
                    q = 2 * n + j
                    to = acc[:, b * NT + c * BC + q, :]
                    last = dve.scalar_tensor_tensor(
                        to, ps_t[m % 2][:, j * D:(j + 1) * D], inv_sum[:, c, q:q + 1],
                        to, ALU.mult, ALU.add)
                last.then_inc(s_bank_free, 1)

        routed = 0

        def step(*instructions):
            nonlocal routed
            for instruction in instructions:
                instruction.then_inc(s_route, 1)
            routed += len(instructions)

        def ready():
            dve.wait_ge(s_route, routed)

        m4 = biased[:, :, :].rearrange("p t (g k) -> p t g k", k=E // G)

        def route(b, stage):
            if stage > 0:
                ready()
            if stage == 0:
                dve.wait_ge(s_x_free, X_SCORES[b])
                step(dve.tensor_tensor(biased[:, :, :], score[:, :, :],
                                       bias_bc[:, :].unsqueeze(1).to_broadcast([P, NT, E]), ALU.add))
            elif stage == 1:
                step(dve.tensor_tensor(pair_a[:, :, :], m4[:, :, :, 0], m4[:, :, :, 1], ALU.max),
                     dve.tensor_tensor(pair_b[:, :, :], m4[:, :, :, 2], m4[:, :, :, 3], ALU.max))
                ready()
                step(dve.tensor_tensor(group[:, :, :], pair_a[:, :, :], pair_b[:, :, :], ALU.add))
                ready()
                step(dve.tensor_tensor(pair_a[:, :, :], m4[:, :, :, 0], m4[:, :, :, 1], ALU.add),
                     dve.tensor_tensor(pair_b[:, :, :], m4[:, :, :, 2], m4[:, :, :, 3], ALU.add))
            elif stage == 2:
                step(dve.tensor_tensor(group[:, :, :], group[:, :, :], pair_a[:, :, :], ALU.max))
                ready()
                step(dve.tensor_tensor(group[:, :, :], group[:, :, :], pair_b[:, :, :], ALU.max))
            elif stage == 3:
                above, level = rank_parts[b]
                other = group[:, :, :].unsqueeze(2).to_broadcast([P, NT, G, G])
                this = group[:, :, :].unsqueeze(3).to_broadcast([P, NT, G, G])
                step(dve.tensor_tensor(above, other, this, ALU.is_gt),
                     dve.tensor_tensor(level, other, this, ALU.is_equal))
            elif stage == 4:
                above, level = rank_parts[b]
                step(dve.tensor_tensor(level, level,
                                       earlier[:, :, :].unsqueeze(1).to_broadcast([P, NT, G, G]),
                                       ALU.mult))
                ready()
                step(dve.tensor_tensor(above, above, level, ALU.add))
            elif stage == 5:
                step(dve.reduce_sum(rank[:, :, :], rank_parts[b][0], AX.X))
                ready()
                step(dve.tensor_scalar(kept[:, :, :], rank[:, :, :], TOPG - 0.5, None, ALU.is_lt))
                ready()
                step(dve.tensor_tensor(m4, m4, kept[:, :, :].unsqueeze(3)
                                       .to_broadcast([P, NT, G, E // G]), ALU.mult))
            elif stage == 6:
                step(dve.tensor_scalar(biased[:, :, :], biased[:, :, :], 0.0, None, ALU.add))
                ready()
                step(*[dve.max(best[:, t, :], biased[:, t, :]) for t in range(NT)])
            elif stage == 7:
                step(*[dve.match_replace(taken[:, t, :], best[:, t, :], biased[:, t, :], NEVER)
                       for t in range(NT)])
            elif stage == 8:
                step(dve.tensor_scalar(taken[:, :, :], taken[:, :, :], NEVER, None, ALU.is_equal))
                ready()
                step(dve.tensor_tensor(taken[:, :, :], taken[:, :, :], score[:, :, :], ALU.mult))
                ready()
                step(dve.reduce_sum(total[:, :], taken[:, :, :], AX.X))
            elif stage == 9:
                step(dve.tensor_scalar(total[:, :], total[:, :], 1e-20, None, ALU.add))
                ready()
                step(dve.reciprocal(inv_total[:, :], total[:, :]))
                ready()
                step(dve.tensor_scalar(inv_total[:, :], inv_total[:, :], SCALE, None, ALU.mult))
                ready()
                step(dve.tensor_tensor(coeff[:, :, :], taken[:, :, :],
                                       inv_total[:, :].unsqueeze(2).to_broadcast([P, NT, E]), ALU.mult))
            else:
                if b > 0:
                    dve.wait_ge(s_co_dram, 16 * (B * NC + 4 * b))
                dve.transpose(flat(coT), flat(coeff)).then_inc(s_coT, 1)

        def low(slot, u):
            dve.wait_ge(s_h_hi, u + 1)
            dve.tensor_tensor(h_lo[slot], h[slot % 2][:, :], h_hi[slot].bitcast(F32),
                              ALU.subtract).then_inc(s_h_lo, 1)

        def unit(slot, u, pairs, first=False):
            c = slot % NC
            dve.wait_ge(s_silu, u + 1)
            dve.tensor_tensor(gated[c], sg[c], ps_gu[c][1], ALU.mult).then_inc(s_gu_free, 1)
            if not first:
                low((slot - 1) % HB, u - 1)
            dve.wait_ge(s_gu_free, u + GUF0 + 1)
            dve.wait_ge(s_co_in[slot // NC], 16 * pairs + 16)
            dve.tensor_tensor(h[c][:, :], gated[c], co[slot // NC][:, c * NQ:(c + 1) * NQ],
                              ALU.mult).then_inc(s_h, 1)

        for kind, k, n, m in walk(START):
            bank = [ps_x, ps_z][(m or 0) % 2]
            if kind == "N":
                norm(k, n)
            elif kind == "Y":
                xn_low(k, n, bank, m)
            elif kind == "X":
                project(k, bank, m)
            elif kind == "R":
                maximum(n, n)
        dve.wait_ge(s_in, 32)
        dve.wait_ge(s_const, CONSTS)

        def pair(b, p, order, x_before):
            for kind, k, n, m in walk(order):
                if kind == "N":
                    if n == 0 and order is LAST_PAIR and k >= NC:
                        use = count_of(order, ("W", k, 1)) + 1
                        dve.wait_ge(s_bank_free, BANK0 + p * BANKED + use)
                    norm(norm_of(order, k), n)
                elif kind == "X":
                    project(k, ps_x, x_before + m)
                elif kind == "Y":
                    xn_low(k, n, bank_of(order, kind, k, n), x_before + m)
                elif kind == "L":
                    dve.wait_ge(s_x_hi, x_before + m + 1)
                    part = expT[:, n * NQ:(n + 1) * NQ]
                    dve.tensor_scalar(part, part, 1.0, None, ALU.add).then_inc(s_x_free, 1)
                elif kind == "M":
                    dve.wait_ge(s_x_hi, x_before + m + 1)
                    dve.reciprocal(flat(score), flat(score)).then_inc(s_x_free, 1)
                elif kind == "G":
                    route(k, n)
                elif kind == "U":
                    unit(k % HB, k, k // BU, k == 0)
                else:
                    attend(kind, k, n, m, b, p)

        each_pair(dve, pair)

        def copy_out(b, c):
            dve.wait_ge(s_dn, (b + 1) * UNITS - NC + c + 1 + DN0)
            dve.tensor_copy(oT[:, 1, c * NQ:(c + 1) * NQ], ps_o[c][1]).then_inc(s_oT_dve, 1)

        def add_out(b, c):
            for half in range(2):
                t = b * NT + c * BC + half * 2
                dve.wait_ge(s_oT_ps, b * 2 * NC + 2 * c + half + 1)
                to = acc[:, t:t + 2, :].rearrange("p t d -> p (t d)")
                dve.tensor_tensor(to, ps_o[c][half], to, ALU.add).then_inc(s_final, 1)

        def body(b, i):
            for j in range(BU):
                unit((j + NC) % HB, b * UNITS + i * BU + j + NC, b * BODIES + i + (j + NC) // BU)

        with dve.Fori(DONE_BODIES, BODIES - 1) as i:
            body(0, i)
        last = UNITS - NC
        for j in range(NC):
            unit(j + NC, last + j, BODIES - 1)
        for c in range(NC):
            unit(c, UNITS + c, BODIES)
            copy_out(0, c)
        for c in range(NC):
            add_out(0, c)
        with dve.Fori(0, BODIES - 1) as i:
            body(1, i)
        for j in range(NC):
            unit(j + NC, UNITS + last + j, 2 * BODIES - 1, j > 0)
            low(j + NC, UNITS + last + j)
        for c in range(NC):
            copy_out(1, c)
        for c in range(NC):
            add_out(1, c)


def kernel(**inputs):
    import concourse.bacc as bacc
    from concourse.bass_utils import run_bass_kernel_spmd

    def by_chunk(w):
        w = np.swapaxes(w, -1, -2)
        w = w.reshape(*w.shape[:-2], ND, P, w.shape[-1])
        return np.swapaxes(w, -3, -2)

    a = {k: np.asarray(v) for k, v in inputs.items()}
    wq, wk, wv = (by_chunk(a["L0_attn_W_" + n]) for n in "QKV")
    first = [w[0::2].reshape(PAIRS, P, ND * DH) for w in (wq, wk)]
    second = [w[1::2].reshape(PAIRS, P, ND * DH) for w in (wq, wk)]
    v2 = wv.reshape(PAIRS, 2, P, ND, DH).transpose(0, 2, 3, 1, 4).reshape(PAIRS, P, ND * 2 * DH)
    wo = a["L0_attn_W_O"].reshape(D, H, DH).transpose(1, 2, 0)

    def shared(w):
        return w.reshape(SI // I, I, D)

    gate = by_chunk(np.concatenate([a["L0_ffn_gate_proj"], shared(a["L0_ffn_shared_gate"])]))
    up = by_chunk(np.concatenate([a["L0_ffn_up_proj"], shared(a["L0_ffn_shared_up"])]))
    down = np.concatenate([a["L0_ffn_down_proj"].transpose(0, 2, 1),
                           shared(a["L0_ffn_shared_down"].T)])
    arrays = {
        "x": a["L0_attn_x"],
        "w_a": np.concatenate(first + [v2], axis=2),
        "w_b": np.concatenate(second, axis=2),
        "w_o": wo,
        "router": by_chunk(a["L0_ffn_router_weight"]),
        "bias": a["L0_ffn_e_score_correction_bias"],
        "experts": np.concatenate([gate.reshape(EX, P, ND * I), up.reshape(EX, P, ND * I), down],
                                  axis=2),
    }
    arrays = {f"{k}_dram": np.ascontiguousarray(v) for k, v in arrays.items()}
    nc = bacc.Bacc("TRN2", target_bir_lowering=False, num_devices=1)
    args = [nc.dram_tensor(k, v.shape, mybir.dt.from_np(v.dtype), kind="ExternalInput").ap()
            for k, v in arrays.items()]
    out = nc.dram_tensor("out_dram", (B, S, D), F32, kind="ExternalOutput").ap()
    layer(nc, *args, out)
    r = run_bass_kernel_spmd(nc, [arrays], core_ids=[0])
    return r.results[0]["out_dram"]
```
